# Optimizing a Trainium2 kernel written in Bass

```python
import numpy as np
import jax
import jax.numpy as jnp

def _softmax(x, axis=-1):
    return jax.nn.softmax(x, axis=axis)

def _gelu(x):
    return jax.nn.gelu(x, approximate=True)

def _silu(x):
    return jax.nn.silu(x)

def _sigmoid(x):
    return jax.nn.sigmoid(x)

def _layernorm(x, axis=-1, eps=1e-05):
    m = jnp.mean(x, axis=axis, keepdims=True)
    v = jnp.var(x, axis=axis, keepdims=True)
    return (x - m) / jnp.sqrt(v + eps)

def _scatter_add(tgt, idx, src, axis=0):
    return tgt.at[idx].add(src)

def _segment_sum(src, seg, n):
    return jax.ops.segment_sum(src, seg, n)
kernel_name = 'mk_vit_tower_d1_tok_img768_r4_92568a'

def setup_inputs(seed: int=0):
    np.random.seed(seed)
    _w = jnp.asarray

    def _rec_inputs():
        import jax
        import jax.numpy as jnp
        _rk = jax.random.key(seed)
        x = -0.000596345 + 1.00056 * jax.random.normal(jax.random.fold_in(_rk, 1), (16, 3, 64, 64), jnp.float32)
        return x
    x = _rec_inputs()

    def _L0_tok_setup():
        import jax, jax.numpy as jnp
        import numpy as np
        B = 16
        IMG = 64
        CH = 3
        EMBED = 64
        GP = 16
        PRE = [1, 2, 4]
        N_LEVELS = 3
        FUSED = EMBED * N_LEVELS

        def hilbert_flat_indices(n):
            t = np.arange(n * n, dtype=np.int64)
            x = np.zeros(n * n, dtype=np.int64)
            y = np.zeros(n * n, dtype=np.int64)
            s = 1
            while s < n:
                rx = 1 & t // 2
                ry = 1 & (t ^ rx)
                swap = ry == 0
                flip = swap & (rx == 1)
                x = np.where(flip, s - 1 - x, x)
                y = np.where(flip, s - 1 - y, y)
                x2 = np.where(swap, y, x)
                y2 = np.where(swap, x, y)
                x, y = (x2, y2)
                x = x + s * rx
                y = y + s * ry
                t = t // 4
                s *= 2
            return y * n + x

        def _level(x, idx, W, b, p, gp):
            Bsz, C, H, _ = x.shape
            h = H // p
            t = x.reshape(Bsz, C, h, p, h, p).transpose(0, 2, 4, 3, 5, 1).reshape(Bsz, h * h, p * p * C)
            t = t[:, idx]
            t = t.reshape(Bsz, h * h // gp, gp * p * p * C)
            return t @ W.T + b

        def _interp_linear(x, n_out):
            L = x.shape[1]
            pos = (jnp.arange(n_out, dtype=jnp.float32) + 0.5) * (L / n_out) - 0.5
            pos = jnp.clip(pos, 0.0, L - 1)
            i0 = jnp.floor(pos).astype(jnp.int32)
            i1 = jnp.minimum(i0 + 1, L - 1)
            w = (pos - i0).astype(x.dtype)
            return x[:, i0] * (1.0 - w)[None, :, None] + x[:, i1] * w[None, :, None]
        key = jax.random.key(seed)
        ks = jax.random.split(key, 9)
        inp = {'x': jax.random.normal(ks[0], (B, CH, IMG, IMG), jnp.float32)}
        for i, p in enumerate(PRE):
            din = CH * p * p * GP
            inp[f'W{i}'] = jax.random.normal(ks[1 + 2 * i], (EMBED, din), jnp.float32) * din ** (-0.5)
            inp[f'b{i}'] = jax.random.normal(ks[2 + 2 * i], (EMBED,), jnp.float32) * 0.02
        inp['Wf'] = jax.random.normal(ks[7], (FUSED, FUSED), jnp.float32) * FUSED ** (-0.5)
        inp['bf'] = jax.random.normal(ks[8], (FUSED,), jnp.float32) * 0.02
        for i, p in enumerate(PRE):
            inp[f'idx{i}'] = jnp.asarray(hilbert_flat_indices(IMG // p), jnp.int32)
        return inp
    _L0_tok_all = _L0_tok_setup()
    _L0_tok_in = {k: v for k, v in _L0_tok_all.items() if k in ('W0', 'b0', 'W1', 'b1', 'W2', 'b2', 'Wf', 'bf', 'idx0', 'idx1', 'idx2')}
    del _L0_tok_all

    def _L0_attn_setup():
        import jax, jax.numpy as jnp
        import numpy as np
        HEADS = 12
        EPS = 1e-06

        def _rfm_softmax(seq, omega, query):
            d = seq.shape[-1]
            F = omega.shape[0]
            s = seq * float(d) ** (-0.25)
            s = jnp.einsum('bhld,fd->bhlf', s, omega)
            diag = jnp.sum(s, axis=-1, keepdims=True) / 2.0
            if query:
                m = jnp.max(s, axis=-1, keepdims=True)
            else:
                m = jnp.max(s, axis=(1, 3), keepdims=True)
            return float(F) ** (-0.5) * (jnp.exp(s - diag - m) + EPS)
        key = jax.random.key(seed)
        ks = jax.random.split(key, 5)
        B, L, E, F = (8, 128, 192, 64)
        Dh = E // HEADS
        x = jax.random.normal(ks[0], (B, L, E), dtype=jnp.float32)
        w_inp = jax.random.normal(ks[1], (1, E, 3 * E), dtype=jnp.float32) * 0.02
        b_inp = jnp.zeros((3 * E,), jnp.float32)
        w_out = jax.random.normal(ks[2], (1, E, E), dtype=jnp.float32) * 0.02
        b_out = jnp.zeros((E,), jnp.float32)
        g = jax.random.normal(ks[3], (Dh, F), dtype=jnp.float32)
        q, _ = jnp.linalg.qr(g)
        omega = q.T[:F].astype(jnp.float32)
        return {'x': x, 'w_inp': w_inp, 'b_inp': b_inp, 'w_out': w_out, 'b_out': b_out, 'omega': omega}
    _L0_attn_all = _L0_attn_setup()
    _L0_attn_in = {k: v for k, v in _L0_attn_all.items() if k in ('w_inp', 'b_inp', 'w_out', 'b_out', 'omega')}
    del _L0_attn_all

    def _L0_ffn_setup():
        import jax, jax.numpy as jnp
        import numpy as np
        B, N, D, E, F, K = (2, 512, 192, 8, 768, 2)
        V_MAX = 3.0
        FEAT_CLAMP = 10.0

        def bk_green_diag(a):
            aT = jnp.swapaxes(a, 0, 1)

            def step(c, ai):
                d = ai - 1.0 / c
                return (d, d)
            d0 = aT[0]
            _, d_rest = jax.lax.scan(step, d0, aT[1:])
            d = jnp.concatenate([d0[None], d_rest], axis=0)
            eN = aT[-1]
            _, e_rest = jax.lax.scan(step, eN, aT[:-1], reverse=True)
            e = jnp.concatenate([e_rest, eN[None]], axis=0)
            G = 1.0 / (d + e - aT)
            return jnp.swapaxes(G, 0, 1)
        key = jax.random.key(seed)
        ks = jax.random.split(key, 8)
        s = lambda k, shape, sc: jax.random.normal(k, shape, jnp.float32) * sc
        return {'x': s(ks[0], (B, N, D), 1.0), 'v_w': s(ks[1], (D,), 0.02), 'v_b': jnp.zeros((), jnp.float32), 'gate_w': s(ks[2], (D, E), 0.02), 'gate_b': jnp.zeros((E,), jnp.float32), 'w1': s(ks[3], (E, D, F), 0.02), 'b1': jnp.zeros((E, F), jnp.float32), 'w2': s(ks[4], (E, F, D), 0.02), 'b2': jnp.zeros((E, D), jnp.float32), 'out_w': s(ks[5], (2, D), 0.02), 'out_b': jnp.zeros((D,), jnp.float32), 'bk_scale': jnp.ones((D,), jnp.float32)}
    _L0_ffn_all = _L0_ffn_setup()
    _L0_ffn_in = {k: v for k, v in _L0_ffn_all.items() if k in ('v_w', 'v_b', 'gate_w', 'gate_b', 'w1', 'b1', 'w2', 'b2', 'out_w', 'out_b', 'bk_scale')}
    del _L0_ffn_all
    return {'x': x, 'L0_tok_W0': _L0_tok_in['W0'], 'L0_tok_b0': _L0_tok_in['b0'], 'L0_tok_W1': _L0_tok_in['W1'], 'L0_tok_b1': _L0_tok_in['b1'], 'L0_tok_W2': _L0_tok_in['W2'], 'L0_tok_b2': _L0_tok_in['b2'], 'L0_tok_Wf': _L0_tok_in['Wf'], 'L0_tok_bf': _L0_tok_in['bf'], 'L0_tok_idx0': _L0_tok_in['idx0'], 'L0_tok_idx1': _L0_tok_in['idx1'], 'L0_tok_idx2': _L0_tok_in['idx2'], 'L0_attn_w_inp': _L0_attn_in['w_inp'], 'L0_attn_b_inp': _L0_attn_in['b_inp'], 'L0_attn_w_out': _L0_attn_in['w_out'], 'L0_attn_b_out': _L0_attn_in['b_out'], 'L0_attn_omega': _L0_attn_in['omega'], 'L0_ffn_v_w': _L0_ffn_in['v_w'], 'L0_ffn_v_b': _L0_ffn_in['v_b'], 'L0_ffn_gate_w': _L0_ffn_in['gate_w'], 'L0_ffn_gate_b': _L0_ffn_in['gate_b'], 'L0_ffn_w1': _L0_ffn_in['w1'], 'L0_ffn_b1': _L0_ffn_in['b1'], 'L0_ffn_w2': _L0_ffn_in['w2'], 'L0_ffn_b2': _L0_ffn_in['b2'], 'L0_ffn_out_w': _L0_ffn_in['out_w'], 'L0_ffn_out_b': _L0_ffn_in['out_b'], 'L0_ffn_bk_scale': _L0_ffn_in['bk_scale']}

def reference(x, L0_tok_W0, L0_tok_b0, L0_tok_W1, L0_tok_b1, L0_tok_W2, L0_tok_b2, L0_tok_Wf, L0_tok_bf, L0_tok_idx0, L0_tok_idx1, L0_tok_idx2, L0_attn_w_inp, L0_attn_b_inp, L0_attn_w_out, L0_attn_b_out, L0_attn_omega, L0_ffn_v_w, L0_ffn_v_b, L0_ffn_gate_w, L0_ffn_gate_b, L0_ffn_w1, L0_ffn_b1, L0_ffn_w2, L0_ffn_b2, L0_ffn_out_w, L0_ffn_out_b, L0_ffn_bk_scale):
    import jax
    import jax.numpy as jnp

    def _L0_tok_ref(x, W0, b0, W1, b1, W2, b2, Wf, bf, idx0, idx1, idx2):
        import jax, jax.numpy as jnp
        import numpy as np
        B = 16
        IMG = 64
        CH = 3
        EMBED = 64
        GP = 16
        PRE = [1, 2, 4]
        N_LEVELS = 3
        FUSED = EMBED * N_LEVELS

        def hilbert_flat_indices(n):
            t = np.arange(n * n, dtype=np.int64)
            x = np.zeros(n * n, dtype=np.int64)
            y = np.zeros(n * n, dtype=np.int64)
            s = 1
            while s < n:
                rx = 1 & t // 2
                ry = 1 & (t ^ rx)
                swap = ry == 0
                flip = swap & (rx == 1)
                x = np.where(flip, s - 1 - x, x)
                y = np.where(flip, s - 1 - y, y)
                x2 = np.where(swap, y, x)
                y2 = np.where(swap, x, y)
                x, y = (x2, y2)
                x = x + s * rx
                y = y + s * ry
                t = t // 4
                s *= 2
            return y * n + x

        def _level(x, idx, W, b, p, gp):
            Bsz, C, H, _ = x.shape
            h = H // p
            t = x.reshape(Bsz, C, h, p, h, p).transpose(0, 2, 4, 3, 5, 1).reshape(Bsz, h * h, p * p * C)
            t = t[:, idx]
            t = t.reshape(Bsz, h * h // gp, gp * p * p * C)
            return t @ W.T + b

        def _interp_linear(x, n_out):
            L = x.shape[1]
            pos = (jnp.arange(n_out, dtype=jnp.float32) + 0.5) * (L / n_out) - 0.5
            pos = jnp.clip(pos, 0.0, L - 1)
            i0 = jnp.floor(pos).astype(jnp.int32)
            i1 = jnp.minimum(i0 + 1, L - 1)
            w = (pos - i0).astype(x.dtype)
            return x[:, i0] * (1.0 - w)[None, :, None] + x[:, i1] * w[None, :, None]
        Ws = [(idx0, W0, b0, PRE[0]), (idx1, W1, b1, PRE[1]), (idx2, W2, b2, PRE[2])]
        outs = [_level(x, idx, W, b, p, GP) for idx, W, b, p in Ws]
        n_tokens = outs[0].shape[1]
        outs = [outs[0]] + [_interp_linear(o, n_tokens) for o in outs[1:]]
        y = jnp.concatenate(outs, axis=-1)
        return y @ Wf.T + bf

    def _L0_attn_ref(x, w_inp, b_inp, w_out, b_out, omega):
        import jax, jax.numpy as jnp
        import numpy as np
        HEADS = 12
        EPS = 1e-06

        def _rfm_softmax(seq, omega, query):
            d = seq.shape[-1]
            F = omega.shape[0]
            s = seq * float(d) ** (-0.25)
            s = jnp.einsum('bhld,fd->bhlf', s, omega)
            diag = jnp.sum(s, axis=-1, keepdims=True) / 2.0
            if query:
                m = jnp.max(s, axis=-1, keepdims=True)
            else:
                m = jnp.max(s, axis=(1, 3), keepdims=True)
            return float(F) ** (-0.5) * (jnp.exp(s - diag - m) + EPS)
        B, L, E = x.shape
        H = HEADS
        Dh = E // H
        c = jnp.einsum('ble,eo->blo', x, w_inp[0]) + b_inp
        q, k, v = jnp.split(c, 3, axis=2)
        split = lambda t: t.reshape(B, L, H, Dh).transpose(0, 2, 1, 3)
        q, k, v = (split(q), split(k), split(v))
        qf = _rfm_softmax(q, omega, query=True)
        kf = _rfm_softmax(k, omega, query=False)
        qf = qf.transpose(2, 0, 1, 3)
        kf = kf.transpose(2, 0, 1, 3)
        vl = v.transpose(2, 0, 1, 3)
        rhs = jnp.cumsum(kf[..., None, :] * vl[..., :, None], axis=0)
        a = jnp.einsum('lbhdf,lbhf->lbhd', rhs, qf)
        denom = jnp.einsum('lbhf,lbhf->lbh', qf, jnp.cumsum(kf, axis=0))[..., None]
        a = a / (denom + EPS)
        a = a.transpose(1, 2, 0, 3)
        a = a.transpose(0, 2, 1, 3).reshape(B, L, E)
        out = jnp.einsum('ble,eo->blo', a, w_out[0]) + b_out
        return out

    def _L0_ffn_ref(x, v_w, v_b, gate_w, gate_b, w1, b1, w2, b2, out_w, out_b, bk_scale):
        import jax, jax.numpy as jnp
        import numpy as np
        B, N, D, E, F, K = (2, 512, 192, 8, 768, 2)
        V_MAX = 3.0
        FEAT_CLAMP = 10.0

        def bk_green_diag(a):
            aT = jnp.swapaxes(a, 0, 1)

            def step(c, ai):
                d = ai - 1.0 / c
                return (d, d)
            d0 = aT[0]
            _, d_rest = jax.lax.scan(step, d0, aT[1:])
            d = jnp.concatenate([d0[None], d_rest], axis=0)
            eN = aT[-1]
            _, e_rest = jax.lax.scan(step, eN, aT[:-1], reverse=True)
            e = jnp.concatenate([e_rest, eN[None]], axis=0)
            G = 1.0 / (d + e - aT)
            return jnp.swapaxes(G, 0, 1)
        v = jnp.clip(x @ v_w + v_b, -V_MAX, V_MAX)
        a = (-2.0 + v).astype(jnp.complex64) - 1j
        G = bk_green_diag(a)
        feats = jnp.stack([G.real, G.imag], axis=-1)
        logits = x @ gate_w + gate_b
        probs = jax.nn.softmax(logits, axis=-1)
        topv, topi = jax.lax.top_k(probs, K)
        topv = topv / jnp.sum(topv, axis=-1, keepdims=True)
        comb = jnp.sum(topv[..., None] * jax.nn.one_hot(topi, E, dtype=x.dtype), axis=2)
        h = jax.nn.gelu(jnp.einsum('bnd,edf->bnef', x, w1) + b1)
        y = jnp.einsum('bnef,efd->bned', h, w2) + b2
        ffn_out = jnp.einsum('bne,bned->bnd', comb, y)
        feats_c = jnp.clip(feats, -FEAT_CLAMP, FEAT_CLAMP)
        spec_out = feats_c @ out_w + out_b
        return ffn_out + bk_scale * spec_out
    h = _L0_tok_ref(x, L0_tok_W0, L0_tok_b0, L0_tok_W1, L0_tok_b1, L0_tok_W2, L0_tok_b2, L0_tok_Wf, L0_tok_bf, L0_tok_idx0, L0_tok_idx1, L0_tok_idx2)
    h = h + _L0_attn_ref(_layernorm(h, axis=-1), L0_attn_w_inp, L0_attn_b_inp, L0_attn_w_out, L0_attn_b_out, L0_attn_omega)
    h = h + _L0_ffn_ref(_layernorm(h, axis=-1), L0_ffn_v_w, L0_ffn_v_b, L0_ffn_gate_w, L0_ffn_gate_b, L0_ffn_w1, L0_ffn_b1, L0_ffn_w2, L0_ffn_b2, L0_ffn_out_w, L0_ffn_out_b, L0_ffn_bk_scale)
    return h

_drawn_inputs = setup_inputs


def setup_inputs(seed=0):
    import zlib

    import numpy as np

    out = dict(_drawn_inputs(seed))
    spreads = {'L0_attn_b_inp': (0.0, 0.1),
     'L0_attn_b_out': (0.0, 0.1),
     'L0_ffn_gate_b': (0.0, 0.1),
     'L0_ffn_b1': (0.0, 0.311),
     'L0_ffn_b2': (0.0, 0.1),
     'L0_ffn_out_b': (0.0, 0.1),
     'L0_ffn_bk_scale': (1.0, 0.6)}
    factors = {'L0_tok_b0': 3.881,
     'L0_tok_b1': 3.822,
     'L0_tok_b2': 3.069,
     'L0_attn_omega': 8.0,
     'L0_ffn_v_w': 8.0,
     'L0_ffn_out_w': 4.325}
    for name, (base, spread) in spreads.items():
        noise = np.random.default_rng([zlib.crc32(name.encode()), seed]).standard_normal(out[name].shape)
        drawn = base * np.exp(spread * noise) if base else spread * noise
        out[name] = jnp.asarray(drawn.astype(out[name].dtype))
    for name, factor in factors.items():
        out[name] = (out[name] * factor).astype(out[name].dtype)
    return out
```

```python
from contextlib import ExitStack

import numpy as np

import concourse.bass as bass
from concourse import mybir

F32, F32R, BF16 = mybir.dt.float32, mybir.dt.float32r, mybir.dt.bfloat16
U32, I32 = mybir.dt.uint32, mybir.dt.int32
ALU = mybir.AluOpType
ACT = mybir.ActivationFunctionType
AX = mybir.AxisListType.X

P = 128
B, T, D = 16, 256, 192
NT = B * T // P
TJ = T // P
KH = D // 2
EMB = 64
H, DH, NF = 12, 16, 16
HW = NF + 1
VW = DH + 1
GH = 4
NG = H // GH
NE, FF = 8, 768
REGION = B * T + P
NSLOT = NE * REGION + P
XW = D + EMB
ROW = XW + 2
NTILE = 2 * B * T // P + NE - 1
EPS_F, EPS_LN = 1e-6, 1e-5
V_MAX, FEAT_CLAMP = 3.0, 10.0


def upsampling(n_in):
    pos = (np.arange(T, dtype=np.float32) + np.float32(0.5)) * np.float32(n_in / T) - np.float32(0.5)
    pos = np.clip(pos, 0.0, n_in - 1).astype(np.float32)
    i0 = np.floor(pos).astype(np.int32)
    i1 = np.minimum(i0 + 1, n_in - 1)
    w = (pos - i0).astype(np.float32)
    a = np.zeros((n_in, T), np.float32)
    np.add.at(a, (i0, np.arange(T)), np.float32(1) - w)
    np.add.at(a, (i1, np.arange(T)), w)
    return a


def wait_apart(eng, sem, value):
    eng.wait_ge(sem, value)
    eng.nop(nofuse=True)


def tokens_block(nc, a, ident, h_dram):
    with ExitStack() as ctx:
        sb = lambda n, s, d=F32: ctx.enter_context(nc.sbuf_tensor("t_" + n, s, d))
        sem = lambda n: ctx.enter_context(nc.semaphore(n))
        idx = sb("idx", [P, 42], U32)
        g0 = sb("g0", [P, 2, 16, 48])
        g1 = sb("g1", [P, 8, B, 12])
        g2 = sb("g2", [P, 2, B, 48])
        r0 = sb("r0", [P, 2, B, 16, 3])
        r1 = sb("r1", [P, B, 8, 12])
        t0 = sb("t0", [48, B, 2, P])
        t1 = sb("t1", [96, B, 2, 64])
        t2 = sb("t2", [48, B, 2, P])
        w0 = sb("w0", [48, EMB])
        w1 = sb("w1", [96, 2, EMB])
        w2 = sb("w2", [48, 16, EMB])
        bias = sb("bias", [EMB, 3])
        fine = sb("fine", [P, B, T])
        mix = sb("mix", [P, B, D])
        up2 = sb("up2", [17, T])
        mix2 = sb("mix2", [17, B, D])
        o1 = sb("o1", [EMB, B * 64])
        o2 = sb("o2", [EMB, B * 16])
        wf1 = sb("wf1", [EMB, D])
        wf2 = sb("wf2", [EMB, D])
        hs = sb("hs", [P, B, TJ, D])
        bank = [ctx.enter_context(nc.psum_tensor(f"tk{i}", [P, 512], F32)) for i in range(8)]

        idx_in, params_in = sem("idx_in"), sem("params_in")
        got0, got1, got2 = sem("got0"), sem("got1"), sem("got2")
        const_ready = sem("ident_ready")
        regrouped0, regrouped1 = sem("regrouped0"), sem("regrouped1")
        group_done, group_out = sem("group_done"), [sem("group_out_v"), sem("group_out_a")]
        h_out = sem("h_out")
        block = ctx.enter_context(nc.Block())

        groups = [("t2", k) for k in range(8)] + [("t1", k) for k in range(4)] + [("t0", k) for k in range(8)]
        groups = groups[:12] + [("p2", 0), ("p1", 0), ("p1", 1)] + groups[12:] + \
            [("z1", b) for b in range(B)] + [("z2", b) for b in range(B)] + \
            [("p0", k) for k in range(8)] + [("h", b) for b in range(B)]
        number = {g: n for n, g in enumerate(groups)}

        def wait_out(eng, *which):
            for par in range(2):
                n = [number[g] for g in which if number[g] % 2 == par]
                if n:
                    eng.wait_ge(group_out[par], max(n) // 2 + 1)

        @block.sync
        def _(sp):
            sp.dma_start(idx[:], a["idx"].bitcast(U32)).then_inc(idx_in, 16)
            for dst, src in ((w2[:], a["w2"]), (w1[:], a["w1"]), (w0[:], a["w0"]), (bias[:], a["tok_b"]),
                             (wf1[:], a["wf"][EMB:2 * EMB]), (wf2[:], a["wf"][2 * EMB:]), (up2[:], a["up2"]),
                             (mix[0:EMB], a["wf"][0:EMB].unsqueeze(1).broadcast_to([EMB, B, D])),
                             (mix2[16:17], a["bf"].unsqueeze(1).broadcast_to([1, B, D])),
                             (fine[EMB:P], a["up1"].unsqueeze(1).broadcast_to([64, B, T]))):
                sp.dma_start(dst, src).then_inc(params_in, 16)
            for b in range(0, B, 4):
                wait_out(sp, ("h", b + 2), ("h", b + 3))
                sp.dma_start(h_dram[:, b:b + 4], hs[:, b:b + 4].rearrange("p b j d -> p b (j d)")).then_inc(h_out, 16)
            sp.wait_ge(h_out, 16 * (B // 4))

        @block.gpsimd
        def _(pool):
            nc.gpsimd.memset(ident[:], 0.0).then_inc(const_ready, 1)
            pool.wait_ge(const_ready, 1)
            nc.gpsimd.affine_select(out=ident[:], in_=ident[:], compare_op=ALU.not_equal, fill=1.0, base=0,
                                    pattern=[[-1, P]], channel_multiplier=1).then_inc(const_ready, 1)
            pool.wait_ge(idx_in, 16)

            def gather(out, src, col, done):
                pool.indirect_dma_start(out=out, out_offset=None, in_=src,
                                        in_offset=bass.IndirectOffsetOnAxis(ap=idx[:, col:col + 1], axis=0)
                                        ).then_inc(done, 16)
            for j in range(2):
                gather(g2[:, j].rearrange("p b q -> p (b q)"), a["x2"], 40 + j, got2)
            for j in range(8):
                gather(g1[:, j].rearrange("p b q -> p (b q)"), a["x1"], 32 + j, got1)
            for t in range(2):
                for j in range(16):
                    gather(g0[:, t, j], a["x0"], t * 16 + j, got0)

        @block.tensor
        def _(pe):
            pe.wait_ge(const_ready, 2)
            for n, (what, k) in enumerate(groups):
                ps = bank[n % 8]
                if n >= 8:
                    pe.wait_ge(group_out[n % 2], (n - 8) // 2 + 1)
                if what == "t2":
                    if k == 0:
                        pe.wait_ge(got2, 32)
                    for m in range(4):
                        b, j = (4 * k + m) // 2, m % 2
                        last = pe.transpose(ps[0:48, m * P:(m + 1) * P], g2[:, j, b], ident[:])
                elif what == "t1":
                    if k == 0:
                        pe.wait_ge(regrouped1, 1)
                    for m in range(4):
                        last = pe.transpose(ps[0:96, m * P:(m + 1) * P], r1[:, 4 * k + m].rearrange("p j q -> p (j q)"), ident[:])
                elif what == "t0":
                    if k == 0:
                        pe.wait_ge(regrouped0, 2)
                    for m in range(4):
                        b, t = (4 * k + m) // 2, m % 2
                        last = pe.transpose(ps[0:48, m * P:(m + 1) * P], r0[:, t, b].rearrange("p j c -> p (j c)"), ident[:])
                elif what == "p2":
                    wait_out(pe, ("t2", 6), ("t2", 7))
                    pe.wait_ge(params_in, 160)
                    v = t2[:].rearrange("q b j (e t) -> q j e b t", e=8)
                    for j in range(16):
                        last = pe.matmul(ps[0:EMB, 0:T], w2[:, j], v[:, j % 2, j // 2], start=j == 0, stop=j == 15)
                elif what == "p1":
                    wait_out(pe, ("t1", 2), ("t1", 3))
                    for j in range(2):
                        last = pe.matmul(ps[0:EMB, :], w1[:, j], t1[:, 8 * k:8 * k + 8, j], start=j == 0, stop=j == 1)
                elif what == "p0":
                    if k == 0:
                        wait_out(pe, ("t0", 6), ("t0", 7))
                    last = pe.matmul(ps[0:EMB, :], w0[:], t0[:, 2 * k:2 * k + 2].rearrange("q b t p -> q (b t p)"),
                                     start=True, stop=True)
                elif what == "z1":
                    if k == 0:
                        wait_out(pe, ("p1", 0), ("p1", 1))
                    last = pe.matmul(ps[EMB:P, 0:D], o1[:, k * 64:(k + 1) * 64], wf1[:], start=True, stop=True)
                elif what == "z2":
                    if k == 0:
                        wait_out(pe, ("p2", 0))
                    last = pe.matmul(ps[0:16, 0:D], o2[:, k * 16:(k + 1) * 16], wf2[:], start=True, stop=True)
                else:
                    wait_out(pe, ("p0", k // 2), ("z1", k), ("z2", k))
                    for j in range(TJ):
                        tok = slice(j * P, (j + 1) * P)
                        pe.matmul(ps[:, j * D:(j + 1) * D], fine[:, k, tok], mix[:, k], start=True, stop=False)
                        last = pe.matmul(ps[:, j * D:(j + 1) * D], up2[:, tok], mix2[:, k], start=False, stop=True)
                last.then_inc(group_done, 1)

        def copy_out(eng, par, copy, add_bias):
            for n, (what, k) in enumerate(groups):
                if n % 2 != par:
                    continue
                ps = bank[n % 8]
                if what == "t2" and k == 6 + par and par == 0:
                    eng.wait_ge(got1, 16 * 8)
                    copy(r1[:], g1[:].rearrange("p j b q -> p b j q")).then_inc(regrouped1, 1)
                if (what, k) in (("p1", 0), ("p1", 1)):
                    eng.wait_ge(got0, 16 * 32)
                    copy(r0[:, par], g0[:, par].rearrange("p j (b c) -> p b j c", c=3)).then_inc(regrouped0, 1)
                eng.wait_ge(group_done, n + 1)
                if what == "t2":
                    ins = copy(t2[:, 2 * k:2 * k + 2].rearrange("q b j p -> q (b j p)"), ps[0:48, :])
                elif what == "t1":
                    ins = copy(t1[:, 4 * k:4 * k + 4].rearrange("q b j p -> q (b j p)"), ps[0:96, :])
                elif what == "t0":
                    ins = copy(t0[:, 2 * k:2 * k + 2].rearrange("q b j p -> q (b j p)"), ps[0:48, :])
                elif what == "p2":
                    eng.wait_ge(params_in, 160)
                    ins = add_bias(o2[:], ps[0:EMB, 0:T], bias[:, 2:3])
                elif what == "p1":
                    eng.wait_ge(params_in, 160)
                    ins = add_bias(o1[:, k * 512:(k + 1) * 512], ps[0:EMB, :], bias[:, 1:2])
                elif what == "p0":
                    ins = add_bias(fine[0:EMB, 2 * k:2 * k + 2].rearrange("e b t -> e (b t)"), ps[0:EMB, :], bias[:, 0:1])
                elif what == "z1":
                    ins = copy(mix[EMB:P, k], ps[EMB:P, 0:D])
                elif what == "z2":
                    ins = copy(mix2[0:16, k], ps[0:16, 0:D])
                else:
                    ins = copy(hs[:, k].rearrange("p j d -> p (j d)"), ps[:, 0:TJ * D])
                ins.then_inc(group_out[par], 1)

        @block.vector
        def _(dve):
            copy_out(dve, 0, lambda o, i: dve.tensor_copy(o, i),
                     lambda o, i, s: dve.tensor_scalar(o, i, s, None, ALU.add))

        @block.scalar
        def _(act):
            copy_out(act, 1, lambda o, i: act.copy(o, i),
                     lambda o, i, s: act.activation(o, i, ACT.Identity, bias=s))


def attention_block(nc, a, keep, h_dram, h2_dram, xs_dram):
    ident, count, pot = keep["ident"], keep["count"], keep["pot"]
    with ExitStack() as ctx:
        sb = lambda n, s, d=F32: ctx.enter_context(nc.sbuf_tensor("a_" + n, s, d))
        ps = lambda n, s: ctx.enter_context(nc.psum_tensor("a_" + n, s, F32))
        sem = lambda n: ctx.enter_context(nc.semaphore(n))
        causal = sb("causal", [P, P])
        before = sb("before", [P, P], BF16)
        ones = sb("ones", [P, P], BF16)
        block_mask = sb("block_mask", [P, GH, VW])
        eps_col = sb("eps_col", [P, 1])
        first = sb("first", [P, NE])
        region = sb("region", [P, NE])
        omega = sb("omega", [KH, H // 2, HW])
        wqk_t = sb("wqk_t", [KH, 4, D + 1])
        wqkv = sb("wqkv", [KH + 1, 2, 2 * H * HW + D])
        w_out = sb("w_out", [KH + 1, 2, D])
        w_gate = sb("w_gate", [KH + 1, 2, NE + 1])
        hb = sb("hb", [P, 4, TJ, D])
        stats, mv, rstd1 = sb("stats", [P, TJ, 6]), sb("mv", [P, TJ, 2]), sb("rstd1", [P, TJ])
        var_eps, minus_half = sb("var_eps", [P, TJ]), sb("minus_half", [P, TJ])
        xn = sb("xn", [P, TJ, D])
        xn_t = sb("xn_t", [KH + 1, 2, T])
        top = sb("top", [P, 2 * H])
        top_k = sb("top_k", [P, 1])
        shift = sb("shift", [P, 2 * H])
        feat = [sb(f"feat{j}", [P, 2 * H, 32]) for j in range(TJ)]
        kf = sb("kf", [P, H, 32])
        values = sb("values", [P, 2, TJ, H, VW])
        qb_t = sb("qb_t", [P, NG, TJ, GH, P])
        qf_t, kf_t = sb("qf_t", [P, NG, P]), sb("kf_t", [P, NG, T])
        state = sb("state", [P, NG, GH * VW])
        masked = [sb(f"masked{i}", [P, GH, P]) for i in range(2)]
        den = sb("den", [P, TJ * H])
        att = sb("att", [P, TJ, D])
        att_t = sb("att_t", [KH + 1, 2, T])
        h2 = sb("h2", [P, 2, TJ, D])
        stats2, mv2, rstd2 = sb("stats2", [P, TJ, 6]), sb("mv2", [P, TJ, 2]), sb("rstd2", [P, TJ])
        xn2 = sb("xn2", [P, TJ, D])
        xn2_t = sb("xn2_t", [KH + 1, 2, T])
        logits = sb("logits", [P, TJ, NE])
        prob, eq, w8 = sb("prob", [P, TJ, NE]), sb("eq", [P, TJ, NE]), sb("w8", [P, TJ, NE])
        pick = [sb(f"pick{k}", [P, TJ, NE]) for k in range(2)]
        m = sb("m", [P, 6, TJ])
        gate = sb("gate", [P, TJ, 2])
        chosen = sb("chosen", [P, TJ, NE], BF16)
        earlier = sb("earlier", [P, TJ, NE], BF16)
        slot_e, slot_f = sb("slot_e", [P, TJ, NE]), sb("slot_f", [P, TJ, 2])
        slot = sb("slot", [P, TJ, 2], U32)
        dest = sb("dest", [P, TJ, 2])
        rows = sb("rows", [P, TJ, 2, ROW])
        R = [ps(f"r{i}", [P, 512]) for i in range(4)]
        S = [ps(f"s{i}", [P, GH, P]) for i in range(2)]
        AB = ps("ab", [P, 512])
        M = ps("misc", [P, 512])

        names = """w_in setup pool_const h_in xn_ready xnT_done xnT_out qk_done v_done v_out top_done shift_done
            feat_raw feat_ready kf_ready qT_done qT_out state_done state_out s_done s_out av_done att_ready attT_done
            attT_out proj_done h2_ready xn2_ready xn2T_done xn2T_out logit_done logit_out logit_max prob_ready
            chosen_ready slots_ready prefix_done rows_ready scattered h2_stored dve_step
            w_done gated tail rows_x rstd1_ready rstd2_ready gate_step count_step place_step""".split()
        s = {n: sem("b_" + n) for n in names}
        block = ctx.enter_context(nc.Block())
        NSETUP = 15

        def sched(eng, emit):
            emit(0, True, False, False)
            emit(1, True, True, False)
            emit(2, True, True, True)
            with eng.Fori(3, B - 1) as i:
                emit(i, True, True, True)
            emit(B - 1, True, True, True)
            emit(B, False, True, True)
            emit(B + 1, False, False, True)

        @block.sync
        def _(sp):
            loads = [(omega[h * NF:(h + 1) * NF, h, 0:NF], a["omega_t"]) for h in range(6)]
            loads += [(wqk_t[:], a["wqk_t"]), (wqkv[:, :, 2 * H * HW:], a["wv"]), (w_out[:], a["w_out"]),
                      (w_gate[:], a["w_gate"]), ]
            sp.wait_ge(s["pool_const"], 1)
            for dst, src in loads:
                sp.dma_start(dst, src).then_inc(s["w_in"], 16)

            def load_h(b):
                sp.dma_start(hb[:, b % 4], h_dram[:, bass.ds(b, 1)].rearrange("p b (j d) -> p (b j) d", j=TJ)
                             ).then_inc(s["h_in"], 16)

            def emit(i, one, two, three):
                if one and not (isinstance(i, int) and i == B - 1):
                    if not isinstance(i, int) or i >= 3:
                        sp.wait_ge(s["h2_ready"], i - 2)
                    sp.wait_ge(s["h_in"], 16 * (i + 1))
                    load_h(i + 1)
                if two:
                    sp.wait_ge(s["h2_ready"], i)
                    if not isinstance(i, int) or i >= 2:
                        sp.wait_ge(s["h2_stored"], 16 * (i - 1))
                    sp.dma_start(h2_dram[:, bass.ds(i - 1, 1)].rearrange("p b (j d) -> p (b j) d", j=TJ),
                                 h2[:, (i + 1) % 2]).then_inc(s["h2_stored"], 16)
            load_h(0)
            sched(sp, emit)
            sp.wait_ge(s["h2_stored"], 16 * B)

        @block.gpsimd
        def _(pool):
            g = nc.gpsimd
            g.memset(omega[:], 0.0).then_inc(s["pool_const"], 1)
            g.memset(causal[:], 1.0).then_inc(s["setup"], 1)
            g.memset(before[:], 1.0).then_inc(s["setup"], 1)
            g.memset(ones[:], 1.0).then_inc(s["setup"], 1)
            g.memset(block_mask[:], 1.0).then_inc(s["setup"], 1)
            g.memset(qb_t[:], 0.0).then_inc(s["setup"], 1)
            g.iota(first[:], [[-1, NE]], base=NE, channel_multiplier=0,
                   allow_small_or_imprecise_dtypes=True).then_inc(s["setup"], 1)
            g.iota(region[:], [[REGION, NE]], base=0, channel_multiplier=0,
                   allow_small_or_imprecise_dtypes=True).then_inc(s["setup"], 1)
            g.iota(dest[:], [[2 * P, TJ], [1, 2]], base=0, channel_multiplier=2,
                   allow_small_or_imprecise_dtypes=True).then_inc(s["setup"], 1)
            g.memset(xn_t[:], 1.0).then_inc(s["setup"], 1)
            g.memset(att_t[:], 1.0).then_inc(s["setup"], 1)
            g.memset(xn2_t[:], 1.0).then_inc(s["setup"], 1)
            g.memset(feat[0][:], 0.0).then_inc(s["setup"], 1)
            g.memset(feat[1][:], 0.0).then_inc(s["setup"], 1)
            g.memset(values[:], 1.0).then_inc(s["setup"], 1)
            g.memset(minus_half[:], -0.5).then_inc(s["setup"], 1)
            pool.wait_ge(s["setup"], NSETUP)
            g.affine_select(out=causal[:], in_=causal[:], compare_op=ALU.is_ge, fill=0.0, base=0,
                            pattern=[[1, P]], channel_multiplier=-1).then_inc(s["setup"], 1)
            g.affine_select(out=before[:], in_=before[:], compare_op=ALU.is_gt, fill=0.0, base=0,
                            pattern=[[1, P]], channel_multiplier=-1).then_inc(s["setup"], 1)
            g.affine_select(out=block_mask[:], in_=block_mask[:], compare_op=ALU.is_ge, fill=0.0, base=0,
                            pattern=[[-32, GH], [0, VW]], channel_multiplier=1).then_inc(s["setup"], 1)
            pool.wait_ge(s["setup"], NSETUP + 3)
            g.affine_select(out=block_mask[:], in_=block_mask[:], compare_op=ALU.is_gt, fill=0.0, base=NF,
                            pattern=[[32, GH], [0, VW]], channel_multiplier=-1).then_inc(s["setup"], 1)

            def rstd(ready, b, mv, out, sem_name, count):
                wait_apart(pool, s[sem_name], count)
                g.tensor_scalar(var_eps[:], mv[:, :, 1], EPS_LN, None, ALU.add).then_inc(s[ready], 1)
                pool.wait_ge(s[ready], 2 * b + 1)
                g.tensor_tensor(out[:], var_eps[:], minus_half[:], ALU.pow).then_inc(s[ready], 1)

            rstd("rstd1_ready", 0, mv, rstd1, "top_done", 4)

            def emit(i, one, two, three):
                if three:
                    if not isinstance(i, int) or i >= 3:
                        pool.wait_ge(s["scattered"], 64 * (i - 2))
                    pool.wait_ge(s["rows_ready"], 2 * (i - 1))
                    wait_apart(pool, s["rows_x"], 4 * (i - 1))
                    for j in range(TJ):
                        for k in range(2):
                            pool.indirect_dma_start(
                                out=xs_dram, in_=rows[:, j, k], in_offset=None,
                                out_offset=bass.IndirectOffsetOnAxis(ap=slot[:, j, k:k + 1], axis=0)
                            ).then_inc(s["scattered"], 16)
                if one:
                    if not (isinstance(i, int) and i == 0):
                        pool.wait_ge(s["state_done"], i)
                    wait_apart(pool, s["feat_ready"], TJ * i + 1)
                    g.tensor_scalar(kf[:], feat[0][:, H:2 * H], EPS_F, None, ALU.add).then_inc(s["kf_ready"], 1)
                if two:
                    rstd("rstd2_ready", i - 1, mv2, rstd2, "tail", 7 * (i - 1) + 6)
                if one and not (isinstance(i, int) and i == B - 1):
                    rstd("rstd1_ready", i + 1, mv, rstd1, "top_done", 13 * (i + 1) + 4)
            sched(pool, emit)
            pool.wait_ge(s["scattered"], 16 * 4 * B)

        @block.tensor
        def _(pe):
            pe.wait_ge(s["w_in"], 160)
            pe.wait_ge(s["dve_step"], 2)
            for half, rows_n in ((0, KH), (1, KH + 1)):
                for n in range(4):
                    last = pe.matmul(R[half][0:rows_n, n * 6 * HW:(n + 1) * 6 * HW],
                                     wqk_t[:, n, half * KH:half * KH + rows_n],
                                     omega[:].rearrange("d h f -> d (h f)"), start=True, stop=True)
            last.then_inc(s["w_done"], 1)
            pe.wait_ge(s["gated"], 2)
            pe.wait_ge(s["setup"], NSETUP + 4)

            def turn(dst, src, n=KH):
                for c in range(2):
                    for j in range(TJ):
                        last = pe.transpose(dst[0:KH, c * T + j * P:c * T + (j + 1) * P],
                                            src[:, j, c * KH:(c + 1) * KH], ident[:])
                return last

            def emit(i, one, two, three):
                start0 = isinstance(i, int) and i == 0
                b = i - 1

                def scores(g):
                    for j in range(TJ):
                        n = 2 * g + j
                        if not (isinstance(i, int) and i == 1) or n >= 2:
                            pe.wait_ge(s["s_out"], 6 * b + n - 1)
                        pe.matmul(S[j][:].rearrange("p h t -> p (h t)"), kf_t[:, g, j * P:(j + 1) * P],
                                  qb_t[:, g, j].rearrange("p h t -> p (h t)"), start=True, stop=True
                                  ).then_inc(s["s_done"], 1)

                def averages(g):
                    for j in range(TJ):
                        o = j * H * VW + g * GH * VW
                        if j == 1:
                            pe.matmul(AB[:, o:o + GH * VW], qf_t[:, g], state[:, g],
                                      start=True, stop=False, skip_group_check=True)
                        pe.wait_ge(s["s_out"], 6 * b + 2 * g + j + 1)
                        for r in range(GH):
                            last = pe.matmul(AB[:, o + r * VW:o + (r + 1) * VW], masked[j][:, r],
                                             values[:, (i + 1) % 2, j, g * GH + r], start=j == 0, stop=True,
                                             skip_group_check=True)
                        last.then_inc(s["av_done"], 1)

                def qk(j):
                    for c in range(2):
                        last = pe.matmul(R[1 + 2 * j][:, 0:2 * H * HW], xn_t[0:KH + c, c, j * P:(j + 1) * P],
                                         wqkv[0:KH + c, c, 0:2 * H * HW], start=c == 0, stop=c == 1)
                    last.then_inc(s["qk_done"], 1)
                    for c in range(2):
                        last = pe.matmul(R[2][:, j * D:(j + 1) * D], xn_t[0:KH + c, c, j * P:(j + 1) * P],
                                         wqkv[0:KH + c, c, 2 * H * HW:], start=c == 0, stop=c == 1)
                    if j == 1:
                        last.then_inc(s["v_done"], 1)

                def turn_features(j, banks):
                    pe.wait_ge(s["feat_ready"], TJ * i + j + 1)
                    for n in range(2):
                        for g in range(NG):
                            last = pe.transpose(R[banks[n]][:, g * P:(g + 1) * P],
                                                feat[j][:, n * H + g * GH:n * H + (g + 1) * GH].rearrange("p h f -> p (h f)"),
                                                ident[:])
                        last.then_inc(s["qT_done"], 1)

                if two:
                    pe.wait_ge(s["kf_ready"], i)
                    pe.wait_ge(s["v_out"], i)
                    if not isinstance(i, int) or i >= 3:
                        pe.wait_ge(s["slots_ready"], i - 3 + 1)
                    for g in range(NG):
                        last = pe.matmul(M[:, g * GH * VW:(g + 1) * GH * VW],
                                         kf[:, g * GH:(g + 1) * GH].rearrange("p h f -> p (h f)"),
                                         values[:, (i + 1) % 2, 0, g * GH:(g + 1) * GH].rearrange("p h v -> p (h v)"),
                                         start=True, stop=True)
                    last.then_inc(s["state_done"], 1)
                if one:
                    pe.wait_ge(s["xn_ready"], i + 1)
                    if not start0:
                        pe.wait_ge(s["qT_out"], 4 * i)
                    turn(R[0], xn).then_inc(s["xnT_done"], 1)
                if two:
                    pe.wait_ge(s["qT_out"], 4 * i)
                    scores(0)
                if one:
                    pe.wait_ge(s["xnT_out"], i + 1)
                    if not isinstance(i, int) or i >= 2:
                        pe.wait_ge(s["logit_out"], i - 1)
                    qk(0)
                if two:
                    pe.wait_ge(s["state_out"], i)
                    if not isinstance(i, int) or i >= 2:
                        pe.wait_ge(s["att_ready"], i - 1)
                    averages(0)
                if two:
                    scores(1)
                if one:
                    qk(1)
                if two:
                    averages(1)
                    scores(2)
                if one:
                    if two:
                        pe.wait_ge(s["s_out"], 6 * b + 6)
                    pe.wait_ge(s["v_out"], i + 1)
                    turn_features(0, (0, 2))
                if two:
                    averages(2)
                    pe.wait_ge(s["att_ready"], i)
                    if one:
                        pe.wait_ge(s["qT_out"], 4 * i + 1)
                    turn(R[0], att).then_inc(s["attT_done"], 1)
                if three:
                    pe.wait_ge(s["chosen_ready"], i - 1)
                    if two:
                        pe.wait_ge(s["state_out"], i)
                    pe.matmul(M[:, 0:TJ * NE], before[:], chosen[:].rearrange("p j e -> p (j e)"), start=True, stop=False)
                    pe.matmul(M[:, 0:TJ * NE], ones[:], earlier[:].rearrange("p j e -> p (j e)"), start=False, stop=True
                              ).then_inc(s["prefix_done"], 1)
                if two:
                    pe.wait_ge(s["attT_out"], i)
                    if one:
                        pe.wait_ge(s["shift_done"], TJ * i + 1)
                    for j in range(TJ):
                        for c in range(2):
                            last = pe.matmul(R[1][:, j * D:(j + 1) * D], att_t[0:KH + c, c, j * P:(j + 1) * P],
                                             w_out[0:KH + c, c], start=c == 0, stop=c == 1)
                    last.then_inc(s["proj_done"], 1)
                if one:
                    pe.wait_ge(s["shift_done"], TJ * i + 2)
                    if two:
                        pe.wait_ge(s["attT_out"], i)
                    else:
                        pe.wait_ge(s["qT_out"], 4 * i + 1)
                    turn_features(1, (3, 0))
                if two:
                    pe.wait_ge(s["xn2_ready"], i)
                    turn(R[1], xn2).then_inc(s["xn2T_done"], 1)
                    pe.wait_ge(s["xn2T_out"], i)
                    if one:
                        pe.wait_ge(s["qT_out"], 4 * i + 2)
                    for j in range(TJ):
                        for c in range(2):
                            last = pe.matmul(R[2][:, j * (NE + 1):(j + 1) * (NE + 1)],
                                             xn2_t[0:KH + c, c, j * P:(j + 1) * P], w_gate[0:KH + c, c],
                                             start=c == 0, stop=c == 1)
                    last.then_inc(s["logit_done"], 1)
            sched(pe, emit)

        @block.scalar
        def _(act):
            act.wait_ge(s["w_done"], 1)
            for half, n in ((0, KH), (1, KH + 1)):
                act.mul(wqkv[0:n, half, 0:2 * H * HW], R[half][0:n, 0:2 * H * HW], float(DH) ** -0.25
                        ).then_inc(s["gated"], 1)
            act.wait_ge(s["setup"], NSETUP + 4)
            act.wait_ge(s["dve_step"], 5)

            def emit(i, one, two, three):
                if three:
                    act.wait_ge(s["logit_max"], i - 1)
                    act.activation(prob[:], logits[:], ACT.Exp).then_inc(s["prob_ready"], 1)
                if one:
                    act.wait_ge(s["xnT_done"], i + 1)
                    act.copy(xn_t[0:KH].rearrange("d c t -> d (c t)"), R[0][0:KH, 0:2 * T]).then_inc(s["xnT_out"], 1)
                    for j in range(TJ):
                        act.wait_ge(s["shift_done"], TJ * i + j + 1)
                        act.activation(feat[j][:, :, 0:NF], feat[j][:, :, 0:NF], ACT.Exp).then_inc(s["feat_ready"], 1)

                def features_out(j, banks):
                    q_t, k_t = [R[banks[n]][:, 0:NG * P].rearrange("p (g t) -> p g t", g=NG) for n in range(2)]
                    act.wait_ge(s["qT_done"], 4 * i + 2 * j + 1)
                    for r in range(GH):
                        own = slice(32 * r, 32 * r + 32)
                        last = act.activation(qb_t[own, :, j, r], q_t[own], ACT.Identity, bias=eps_col[own, 0:1])
                    if j == 1:
                        last = act.activation(qf_t[:], q_t, ACT.Identity, bias=eps_col[:, 0:1])
                    last.then_inc(s["qT_out"], 1)
                    act.wait_ge(s["qT_done"], 4 * i + 2 * j + 2)
                    act.activation(kf_t[:, :, j * P:(j + 1) * P], k_t, ACT.Identity, bias=eps_col[:, 0:1]
                                   ).then_inc(s["qT_out"], 1)
                if one:
                    if two:
                        act.wait_ge(s["av_done"], 6 * i)
                    features_out(0, (0, 2))
                if two:
                    act.wait_ge(s["attT_done"], i)
                    act.copy(att_t[0:KH].rearrange("d c t -> d (c t)"), R[0][0:KH, 0:2 * T]).then_inc(s["attT_out"], 1)
                if one:
                    features_out(1, (3, 0))
                if two:
                    act.wait_ge(s["xn2T_done"], i)
                    act.copy(xn2_t[0:KH].rearrange("d c t -> d (c t)"), R[1][0:KH, 0:2 * T]).then_inc(s["xn2T_out"], 1)
            sched(act, emit)

        @block.vector
        def _(dve):
            v = nc.vector
            steps = [0]

            def then(ins):
                steps[0] += 1
                ins.then_inc(s["dve_step"], 1)
                dve.wait_ge(s["dve_step"], steps[0])
            dve.wait_ge(s["w_in"], 160)
            then(v.tensor_reduce(top[0:KH, 0:6], omega[:, :, 0:NF], AX, ALU.add))
            then(v.tensor_scalar(omega[:, :, NF], top[0:KH, 0:6], 0.5, None, ALU.mult))
            then(v.memset(count[:], 0.0))
            dve.wait_ge(s["setup"], NSETUP + 4)
            then(v.tensor_reduce(eps_col[:], block_mask[:, :, 0], AX, ALU.add))
            then(v.tensor_scalar(eps_col[:], eps_col[:], EPS_F, None, ALU.mult))

            def norm(src, stats, mv, rstd, dst, sem_name, base, done, rstd_ready, b):
                for j in range(TJ):
                    ins = v.bn_stats(stats[:, j], src[:, j])
                    ins.then_inc(s[sem_name], 1)
                wait_apart(dve, s[sem_name], base + 2)
                for j in range(TJ):
                    v.bn_aggr(mv[:, j], stats[:, j]).then_inc(s[sem_name], 1)
                dve.wait_ge(s[rstd_ready], 2 * (b + 1))
                for j in range(TJ):
                    ins = v.tensor_scalar(dst[:, j], src[:, j], mv[:, j, 0:1], rstd[:, j:j + 1], ALU.subtract, ALU.mult)
                    ins.then_inc(s[done], 1) if j else ins.then_inc(s[sem_name], 1)

            def bc(ap, n):
                return ap.unsqueeze(2).broadcast_to([P, ap.shape[1], n])

            def norm1(b, first=False):
                if not first:
                    dve.wait_ge(s["xnT_done"], b)
                wait_apart(dve, s["h_in"], 16 * (b + 1))
                norm(hb[:, b % 4], stats, mv, rstd1, xn, "top_done", 13 * b, "xn_ready",
                     "rstd1_ready", b)

            def feature_scores(i, j):
                sc = R[1 + 2 * j][:, 0:2 * H * HW].rearrange("p (h f) -> p h f", f=HW)
                n = 13 * i + 5 + 4 * j
                dve.wait_ge(s["qk_done"], TJ * i + j + 1)
                v.tensor_reduce(top[:], sc[:, :, 0:NF], AX, ALU.max).then_inc(s["top_done"], 1)
                dve.wait_ge(s["top_done"], n + 1)
                v.tensor_reduce(top_k[:], top[:, H:], AX, ALU.max).then_inc(s["top_done"], 1)
                v.tensor_tensor(shift[:, 0:H], sc[:, 0:H, NF], top[:, 0:H], ALU.add).then_inc(s["top_done"], 1)
                dve.wait_ge(s["top_done"], n + 3)
                v.tensor_scalar(shift[:, H:], sc[:, H:, NF], top_k[:, 0:1], None, ALU.add).then_inc(s["top_done"], 1)
                dve.wait_ge(s["top_done"], n + 4)
                if not (isinstance(i, int) and i == 0):
                    dve.wait_ge(s["qT_done"], 4 * i - 2 + 2 * j)
                    if j == 0:
                        dve.wait_ge(s["kf_ready"], i)
                v.tensor_tensor(feat[j][:, :, 0:NF], sc[:, :, 0:NF], bc(shift[:], NF), ALU.subtract
                                ).then_inc(s["shift_done"], 1)

            def mask(i, n):
                dve.wait_ge(s["s_done"], 6 * (i - 1) + n + 1)
                if not (isinstance(i, int) and i == 1) or n >= 2:
                    dve.wait_ge(s["av_done"], 6 * (i - 1) + n - 1)
                v.tensor_tensor(masked[n % 2][:], S[n % 2][:], causal[:].unsqueeze(1).broadcast_to([P, GH, P]), ALU.mult
                                ).then_inc(s["s_out"], 1)

            def emit(i, one, two, three):
                if two:
                    dve.wait_ge(s["state_done"], i)
                    if not isinstance(i, int) or i >= 2:
                        dve.wait_ge(s["av_done"], 6 * (i - 1))
                    v.tensor_tensor(state[:], M[:, 0:H * VW].rearrange("p (g c) -> p g c", g=NG),
                                    block_mask[:].rearrange("p h v -> p (h v)").unsqueeze(1).broadcast_to([P, NG, GH * VW]),
                                    ALU.mult).then_inc(s["state_out"], 1)
                    mask(i, 0)
                    mask(i, 1)
                if three:
                    choose(i)
                if one:
                    feature_scores(i, 0)
                if two:
                    mask(i, 2)
                    mask(i, 3)
                if one:
                    dve.wait_ge(s["v_done"], i + 1)
                    if not isinstance(i, int) or i >= 2:
                        dve.wait_ge(s["av_done"], 6 * (i - 1))
                    v.tensor_copy(values[:, i % 2, :, :, 0:DH], R[2][:, 0:TJ * D].rearrange("p (j h d) -> p j h d", j=TJ, h=H)
                                  ).then_inc(s["v_out"], 1)
                    feature_scores(i, 1)
                if two:
                    mask(i, 4)
                    mask(i, 5)
                    normalise(i)
                if three:
                    place(i)
                if two:
                    project(i)
                if one and not (isinstance(i, int) and i == B - 1):
                    norm1_next(i)
                if two:
                    gate_logits(i)

            def norm1_next(i):
                norm1(i + 1)

            def normalise(i):
                ab = AB[:, 0:TJ * H * VW].rearrange("p (h v) -> p h v", v=VW)
                n = 7 * (i - 1)
                dve.wait_ge(s["av_done"], 6 * i)
                v.tensor_scalar(den[:], ab[:, :, DH], EPS_F * NF, None, ALU.add).then_inc(s["tail"], 1)
                dve.wait_ge(s["tail"], n + 1)
                v.reciprocal(den[:], den[:]).then_inc(s["tail"], 1)
                dve.wait_ge(s["tail"], n + 2)
                if not isinstance(i, int) or i >= 2:
                    dve.wait_ge(s["attT_done"], i - 1)
                v.tensor_tensor(att[:].rearrange("p j (h d) -> p (j h) d", d=DH), ab[:, :, 0:DH], bc(den[:], DH), ALU.mult
                                ).then_inc(s["att_ready"], 1)

            def project(i):
                par = (i + 1) % 2
                dve.wait_ge(s["proj_done"], i)
                if not isinstance(i, int) or i >= 3:
                    dve.wait_ge(s["h2_stored"], 16 * (i - 2))
                v.tensor_tensor(h2[:, par], hb[:, (i + 3) % 4], R[1][:, 0:TJ * D].rearrange("p (j d) -> p j d", j=TJ), ALU.add
                                ).then_inc(s["h2_ready"], 1)
                if not isinstance(i, int) or i >= 2:
                    dve.wait_ge(s["xn2T_done"], i - 1)
                wait_apart(dve, s["h2_ready"], i)
                norm(h2[:, par], stats2, mv2, rstd2, xn2, "tail", 7 * (i - 1) + 2, "xn2_ready", "rstd2_ready", i - 1)

            def gate_logits(i):
                lg = R[2][:, 0:TJ * (NE + 1)].rearrange("p (j e) -> p j e", j=TJ)
                dve.wait_ge(s["logit_done"], i)
                v.tensor_reduce(m[:, 0], lg[:, :, 0:NE], AX, ALU.max).then_inc(s["gate_step"], 1)
                dve.wait_ge(s["gate_step"], 20 * (i - 1) + 1)
                if not isinstance(i, int) or i >= 2:
                    dve.wait_ge(s["prob_ready"], i - 1)
                v.tensor_tensor(logits[:], lg[:, :, 0:NE], bc(m[:, 0], NE), ALU.subtract).then_inc(s["logit_max"], 1)
                v.tensor_scalar(pot[:, bass.ds(i - 1, 1)].rearrange("p b j -> p (b j)"), lg[:, :, NE], -V_MAX, V_MAX, ALU.max, ALU.min).then_inc(s["logit_out"], 1)

            def choose(i):
                n = [20 * (i - 2) + 1]

                def step(ins):
                    n[0] += 1
                    ins.then_inc(s["gate_step"], 1)
                    dve.wait_ge(s["gate_step"], n[0])
                w = first[:].unsqueeze(1).broadcast_to([P, TJ, NE])
                dve.wait_ge(s["prob_ready"], i - 1)
                step(v.tensor_reduce(m[:, 1], prob[:], AX, ALU.add))
                step(v.reciprocal(m[:, 1], m[:, 1]))
                step(v.tensor_tensor(prob[:], prob[:], bc(m[:, 1], NE), ALU.mult))
                for k in range(2):
                    step(v.tensor_reduce(m[:, 2 + k], prob[:], AX, ALU.max))
                    step(v.tensor_tensor(eq[:], prob[:], bc(m[:, 2 + k], NE), ALU.is_equal))
                    step(v.tensor_tensor(w8[:], eq[:], w, ALU.mult))
                    step(v.tensor_reduce(m[:, 4], w8[:], AX, ALU.max))
                    step(v.tensor_tensor(pick[k][:], w8[:], bc(m[:, 4], NE), ALU.is_equal))
                    if k == 0:
                        step(v.scalar_tensor_tensor(out=prob[:], in0=pick[0][:], scalar=-2.0, in1=prob[:],
                                                    op0=ALU.mult, op1=ALU.add))
                step(v.tensor_tensor(m[:, 5], m[:, 2], m[:, 3], ALU.add))
                step(v.reciprocal(m[:, 5], m[:, 5]))
                for k in range(2):
                    step(v.tensor_tensor(gate[:, :, k], m[:, 2 + k], m[:, 5], ALU.mult))
                v.tensor_copy(earlier[:, 0], count[:]).then_inc(s["gate_step"], 1)
                step_n = n[0] + 1
                v.tensor_tensor(earlier[:, 1], count[:], pick[0][:, 0], ALU.add).then_inc(s["count_step"], 1)
                v.tensor_tensor(chosen[:], pick[0][:], pick[1][:], ALU.add).then_inc(s["count_step"], 1)
                dve.wait_ge(s["gate_step"], step_n)
                dve.wait_ge(s["count_step"], 3 * (i - 2) + 2)
                v.tensor_tensor(earlier[:, 1], earlier[:, 1], pick[1][:, 0], ALU.add).then_inc(s["count_step"], 1)
                dve.wait_ge(s["count_step"], 3 * (i - 2) + 3)
                v.tensor_tensor(count[:], earlier[:, 1], chosen[:, 1], ALU.add).then_inc(s["chosen_ready"], 1)
                dve.wait_ge(s["chosen_ready"], i - 1)

            def place(i):
                n = [6 * (i - 2)]

                def step(ins):
                    n[0] += 1
                    ins.then_inc(s["place_step"], 1)
                    dve.wait_ge(s["place_step"], n[0])
                dve.wait_ge(s["prefix_done"], i - 1)
                v.tensor_tensor(slot_e[:], M[:, 0:TJ * NE].rearrange("p (j e) -> p j e", j=TJ),
                                region[:].unsqueeze(1).broadcast_to([P, TJ, NE]), ALU.add).then_inc(s["slots_ready"], 1)
                dve.wait_ge(s["slots_ready"], i - 1)
                for k in range(2):
                    step(v.tensor_tensor(pick[k][:], pick[k][:], slot_e[:], ALU.mult))
                    step(v.tensor_reduce(slot_f[:, :, k], pick[k][:], AX, ALU.add))
                if not isinstance(i, int) or i >= 3:
                    dve.wait_ge(s["scattered"], 64 * (i - 2))
                v.tensor_copy(slot[:], slot_f[:]).then_inc(s["rows_ready"], 1)
                for k in range(2):
                    v.tensor_copy(rows[:, :, k, 0:D], xn2[:]).then_inc(s["rows_x"], 1)
                    v.tensor_copy(rows[:, :, k, D:XW], xn2[:, :, P:D]).then_inc(s["rows_x"], 1)
                v.tensor_copy(rows[:, :, :, XW].bitcast(U32), dest[:]).then_inc(s["place_step"], 1)
                n[0] += 1
                v.tensor_copy(rows[:, :, :, XW + 1], gate[:]).then_inc(s["place_step"], 1)
                n[0] += 1
                dve.wait_ge(s["place_step"], n[0])
                v.tensor_scalar(dest[:], dest[:], float(2 * T), None, ALU.add).then_inc(s["rows_ready"], 1)

            norm1(0, first=True)
            sched(dve, emit)


def experts_block(nc, a, keep, xs_dram, y_dram, v_dram, g_dram):
    ident, count, pot = keep["ident"], keep["count"], keep["pot"]
    FT = FF // P
    HALF = FF // 2
    LANES = 48
    STEPS = 4
    CHAIN_TILES = -(-(T - 1) // STEPS)
    CHAIN_OPS = 3
    with ExitStack() as ctx:
        sb = lambda n, s, d=F32: ctx.enter_context(nc.sbuf_tensor("e_" + n, s, d))
        ps = lambda n, s: ctx.enter_context(nc.psum_tensor("e_" + n, s, F32))
        sem = lambda n: ctx.enter_context(nc.semaphore(n))
        w1h, w1l = sb("w1h", [P, NE, FF], F32R), sb("w1l", [P, NE, FF], F32R)
        w1s = sb("w1s", [P, NE, FF], F32R)
        w2s = sb("w2s", [P, NE, FT, 2 * D], F32R)
        bias = sb("fbias", [40, FF + D], F32R)
        select = sb("select", [40, NE, P], F32R)
        raw_a, raw_b = sb("raw_a", [P, 2, FF]), sb("raw_b", [P, 2, FF])
        raw_c = sb("raw_c", [P, 2, FT, D])
        raw_bias = sb("raw_bias", [40, FF + D])
        select_f = sb("select_f", [40, NE, P])
        ones = sb("fones", [P, P])
        n_of, n_int = sb("n_of", [P, NE]), sb("n_int", [1, NE], I32)
        tiles_i, tiles_f = sb("tiles_i", [1, NE], I32), sb("tiles_f", [1, NE])
        jump = sb("jump", [1, NE])
        start = sb("start", [1, NE + 1])
        tile_no, past = sb("tile_no", [1, NTILE + 1]), sb("past", [1, NTILE + 1])
        ex_f, row_f = sb("ex_f", [1, NTILE + 1]), sb("row_f", [1, NTILE + 1])
        ex_i, row_i = sb("ex_i", [1, NTILE + 1], I32), sb("row_i", [1, NTILE + 1], I32)
        pad_rows, pad_id = sb("pad_rows", [P, ROW]), sb("pad_id", [P, 1], I32)
        x = sb("x", [P, ROW])
        tag = sb("tag", [P, 4, 2])
        gate = sb("slot_gate", [P, 1])
        where = sb("where", [P, 1], U32)
        xh, xl = sb("xh", [P, 2, P], F32R), sb("xl", [P, 2, P], F32R)
        sel1, sel2 = sb("sel1", [40, P], F32R), sb("sel2", [40, P], F32R)
        hid = sb("hid", [P, FF])
        hh, hl = sb("hh", [P, FT, P], F32R), sb("hl", [P, FT, P], F32R)
        low = sb("low", [P, D])
        y = sb("y", [P, D])
        pot_t = sb("pot_t", [NT, P])
        v = sb("v", [LANES, T])
        sign = sb("sign", [LANES, T])
        chain_a = sb("chain_a", [LANES, STEPS * CHAIN_TILES + 1, 2])
        chain = sb("chain", [LANES, STEPS * CHAIN_TILES + 1, 2])
        square, size = sb("square", [LANES, 2]), sb("size", [LANES, 1])
        next_a = sb("next_a", [LANES, STEPS, 2])
        state = sb("chain_state", [LANES, STEPS, 2])
        back = raw_b[0:B, 0, 0:2 * T].rearrange("p (t c) -> p t c", c=2)
        z = raw_b[0:B, 1, 0:2 * T].rearrange("p (c t) -> p c t", c=2)
        z2 = raw_a[0:B, 0, 0:2 * T].rearrange("p (c t) -> p c t", c=2)
        XT = ps("xt", [P, 2, P])
        HID = ps("hidden", [P, 2, 512])
        HT = ps("ht", [P, 2, 512])
        Y = ps("yp", [P, 512])
        MISC = ps("fmisc", [P, 512])

        names = """raw_in raw_out split_a split_v consts count_done pad_in lanes_in lanes_out table_ready x_in x_turned x_high x_low
            tagged sel1_ready sel2_ready hid_done hid_ready hidT_done hid_high hid_low y_done low_ready y_ready
            y_out where_ready pads_out pot_done pot_ready v_out step chain_step chain_done g_out pool_step
            bias_in dve_setup idle1 idle2 gate_ready chain_kept chain_set""".split()
        s = {n: sem("f_" + n) for n in names}
        load_done = [sem(f"f_load{k}") for k in range(2)]
        v_in = sem("f_v_in")
        block = ctx.enter_context(nc.Block())

        @block.sync
        def _(sp):
            for e in range(NE):
                if e >= 2:
                    sp.wait_ge(s["split_v"], 3 * (e - 1))
                    sp.wait_ge(s["split_a"], 3 * (e - 1))
                done = load_done[e % 2]
                sp.dma_start(raw_a[:, e % 2], a["ew1"][e, 0:P]).then_inc(done, 16)
                sp.dma_start(raw_b[0:EMB, e % 2], a["ew1"][e, P:D]).then_inc(done, 16)
                sp.dma_start(raw_b[EMB:P, e % 2], a["ew1"][e, P:D]).then_inc(done, 16)
                sp.dma_start(raw_c[:, e % 2], a["ew2"][e].rearrange("(f p) d -> p f d", p=P)).then_inc(done, 16)
                if e == 0:
                    sp.wait_ge(s["consts"], 5)
                    for r in (0, 32):
                        sp.dma_start(raw_bias[r:r + NE, 0:FF], a["eb1"]).then_inc(s["bias_in"], 16)
                        sp.dma_start(raw_bias[r:r + NE, FF:], a["eb2"]).then_inc(s["bias_in"], 16)
                if e == 1:
                    sp.wait_ge(s["pot_ready"], 1)
                    sp.dma_start(v_dram, pot_t[:]).then_inc(s["v_out"], 16)
                    sp.wait_ge(s["v_out"], 16)
                    for r in (0, 32):
                        sp.dma_start(v[r:r + B], v_dram.rearrange("(b j) p -> b (j p)", j=TJ)).then_inc(v_in, 16)
                if e == 2:
                    sp.wait_ge(s["table_ready"], 3)
                    sp.wait_ge(s["pool_step"], 6)
                    for n in range(NE):
                        at = sp.value_load(n_int[0:1, n:n + 1], min_val=0, max_val=B * T)
                        sp.dma_start(xs_dram[bass.ds(n * REGION + at, P)], pad_rows[:]).then_inc(s["pads_out"], 16)
                    sp.dma_start(xs_dram[NE * REGION:NSLOT], pad_rows[:]).then_inc(s["pads_out"], 16)
            sp.wait_ge(s["pads_out"], 16 * (NE + 1))

            def load(i):
                at = sp.value_load(row_i[0:1, bass.ds(i, 1)], min_val=0, max_val=NE * REGION)
                sp.dma_start(x[:], xs_dram[bass.ds(at, P)]).then_inc(s["x_in"], 16)
            load(0)
            with sp.Fori(1, NTILE) as i:
                wait_apart(sp, s["x_turned"], i)
                wait_apart(sp, s["tagged"], i)
                load(i)
            sp.wait_ge(s["chain_done"], 1)
            for c in range(2):
                sp.dma_start(g_dram[c], z2[:, c]).then_inc(s["g_out"], 16)
            sp.wait_ge(s["g_out"], 32)

        @block.gpsimd
        def _(pool):
            g = nc.gpsimd
            g.memset(ones[:], 1.0).then_inc(s["consts"], 1)
            g.memset(pad_rows[:], 0.0).then_inc(s["consts"], 1)
            g.memset(raw_bias[:], 0.0).then_inc(s["consts"], 1)
            g.memset(v[:], 0.0).then_inc(s["consts"], 1)
            g.iota(tile_no[:], [[1, NTILE + 1]], base=0, channel_multiplier=0,
                   allow_small_or_imprecise_dtypes=True).then_inc(s["consts"], 1)
            g.iota(pad_id[:], [[0, 1]], base=2 * B * T, channel_multiplier=1).then_inc(s["pool_step"], 1)
            g.memset(select_f[:], 0.0).then_inc(s["pool_step"], 1)
            pool.wait_ge(s["pool_step"], 2)
            for n, off in enumerate((0, 32)):
                g.affine_select(out=select_f[:], in_=select_f[:], compare_op=ALU.not_equal, fill=1.0, base=-off,
                                pattern=[[-1, NE], [0, P]], channel_multiplier=1).then_inc(s["pool_step"], 1)
                pool.wait_ge(s["pool_step"], 3 + n)
            g.tensor_copy(select[:], select_f[:]).then_inc(s["pool_step"], 1)
            g.tensor_copy(pad_rows[:, XW:XW + 1].bitcast(I32), pad_id[:]).then_inc(s["pool_step"], 1)
            pool.wait_ge(s["pool_step"], 6)
            pool.wait_ge(s["table_ready"], 3)

            def tag_tile(i):
                wait_apart(pool, s["x_in"], 16 * (i + 1))
                g.tensor_copy(tag[:, i % 4], x[:, XW:]).then_inc(s["tagged"], 1)

            def choose_bias(i, dst, ready):
                e = pool.value_load(ex_i[0:1, bass.ds(i, 1)], min_val=0, max_val=NE - 1)
                g.tensor_copy(dst[:], select[:, bass.ds(e, 1)].rearrange("k e p -> k (e p)")).then_inc(s[ready], 1)

            def chain_data(i):
                if not isinstance(i, int) or i >= 2:
                    wait_apart(pool, s["chain_step"], CHAIN_OPS * STEPS * (i - 1))
                    g.tensor_copy(chain[:, bass.ds(STEPS * (i - 2) + 1, STEPS)], state[:]).then_inc(s["chain_kept"], 1)
                g.tensor_copy(next_a[:], chain_a[:, bass.ds(STEPS * (i - 1) + 1, STEPS)]).then_inc(s["chain_kept"], 1)

            def emit(i, front, back_, chained=False):
                if front:
                    tag_tile(i + 1)
                if chained:
                    chain_data(i)
                if front and not (isinstance(i, int) and i == NTILE - 1):
                    wait_apart(pool, s["hid_done"], i + 1)
                    choose_bias(i + 1, sel1, "sel1_ready")
                if back_:
                    wait_apart(pool, s["y_done"], i)
                    if not (isinstance(i, int) and i == NTILE):
                        choose_bias(i, sel2, "sel2_ready")
                    if not isinstance(i, int) or i >= 2:
                        wait_apart(pool, s["y_out"], 16 * (i - 1))
                    g.tensor_copy(where[:], tag[:, (i + 3) % 4, 0:1].bitcast(U32)).then_inc(s["where_ready"], 1)
                    pool.wait_ge(s["where_ready"], i)
                    wait_apart(pool, s["y_ready"], i)
                    if not (isinstance(i, int) and i == NTILE):
                        wait_apart(pool, s["tagged"], i + 1)
                        g.tensor_copy(gate[:], tag[:, i % 4, 1:2]).then_inc(s["gate_ready"], 1)
                    pool.indirect_dma_start(out=y_dram, in_=y[:], in_offset=None,
                                            out_offset=bass.IndirectOffsetOnAxis(ap=where[:, 0:1], axis=0)
                                            ).then_inc(s["y_out"], 16)
            tag_tile(0)
            choose_bias(0, sel1, "sel1_ready")
            choose_bias(0, sel2, "sel2_ready")
            pool.wait_ge(s["tagged"], 1)
            g.tensor_copy(gate[:], tag[:, 0, 1:2]).then_inc(s["gate_ready"], 1)
            emit(0, True, False)
            wait_apart(pool, s["chain_set"], 2)
            emit(1, True, True, True)
            with pool.Fori(2, 1 + CHAIN_TILES) as i:
                emit(i, True, True, True)
            wait_apart(pool, s["chain_step"], CHAIN_OPS * STEPS * CHAIN_TILES)
            g.tensor_copy(chain[:, STEPS * (CHAIN_TILES - 1) + 1:], state[:]).then_inc(s["chain_kept"], 1)
            with pool.Fori(1 + CHAIN_TILES, NTILE - 1) as i:
                emit(i, True, True)
            emit(NTILE - 1, False, True)
            emit(NTILE, False, True)
            pool.wait_ge(s["y_out"], 16 * NTILE)

        @block.tensor
        def _(pe):
            pe.wait_ge(s["consts"], 5)
            pe.matmul(MISC[:, 0:NE], ones[:], count[:], start=True, stop=True).then_inc(s["count_done"], 1)
            pe.transpose(XT[0:NT].rearrange("p a b -> p (a b)")[:, 0:P], pot[:].rearrange("p b j -> p (b j)"), ident[:]
                         ).then_inc(s["pot_done"], 1)
            pe.wait_ge(s["split_v"], 3 * NE)
            pe.wait_ge(s["split_a"], 3 * NE + 1)
            pe.wait_ge(s["dve_setup"], 1)
            pe.wait_ge(s["pot_ready"], 1)

            def turn_x(i):
                pe.wait_ge(s["x_in"], 16 * (i + 1))
                if not (isinstance(i, int) and i == 0):
                    pe.wait_ge(s["x_low"], i)
                pe.transpose(XT[:, 0], x[:, 0:P], ident[:])
                pe.transpose(XT[:, 1], x[:, P:XW], ident[:]).then_inc(s["x_turned"], 1)
            turn_x(0)

            def emit(i, front, back_, last):
                if front:
                    e = pe.value_load(ex_i[0:1, bass.ds(i, 1)], min_val=0, max_val=NE - 1)
                    pe.wait_ge(s["x_high"], i + 1)
                    pe.wait_ge(s["x_low"], i + 1)
                    pe.wait_ge(s["sel1_ready"], i + 1)
                    if not (isinstance(i, int) and i == 0):
                        pe.wait_ge(s["hid_ready"], i)
                    for n in range(2):
                        o, c = HID[:, n, 0:HALF], slice(n * HALF, (n + 1) * HALF)
                        w = lambda t, k=P: t[0:k, bass.ds(e, 1), c].rearrange("p e f -> p (e f)")
                        pe.matmul(o, xh[:, 0], w(w1h), start=True, stop=False)
                        pe.matmul(o, xh[:, 0], w(w1l), start=False, stop=False)
                        pe.matmul(o, xl[:, 0], w(w1h), start=False, stop=False)
                        pe.matmul(o, xh[:, 1], w(w1s), start=False, stop=False)
                        pe.matmul(o, xl[0:EMB, 1], w(w1s, EMB), start=False, stop=False)
                        mm = pe.matmul(o, sel1[:], bias[:, c], start=False, stop=True)
                    mm.then_inc(s["hid_done"], 1)
                    if not last:
                        turn_x(i + 1)
                if back_:
                    e = pe.value_load(ex_i[0:1, bass.ds(i - 1, 1)], min_val=0, max_val=NE - 1)
                    pe.wait_ge(s["hid_high"], i)
                    pe.wait_ge(s["hid_low"], i)
                    pe.wait_ge(s["sel2_ready"], i)
                    if not isinstance(i, int) or i >= 2:
                        pe.wait_ge(s["y_ready"], i - 1)
                    w = lambda f, n: w2s[:, bass.ds(e, 1), f, 0:n].rearrange("p e d -> p (e d)")
                    for f in range(FT):
                        pe.matmul(Y[:, 0:2 * D], hh[:, f], w(f, 2 * D), start=f == 0, stop=False, skip_group_check=True)
                        pe.matmul(Y[:, 0:D], hl[:, f], w(f, D), start=False, stop=False, skip_group_check=True)
                    pe.matmul(Y[:, 0:D], sel2[:], bias[:, FF:], start=False, stop=True, skip_group_check=True
                              ).then_inc(s["y_done"], 1)
                if front:
                    pe.wait_ge(s["hid_ready"], i + 1)
                    if not (isinstance(i, int) and i == 0):
                        pe.wait_ge(s["hid_low"], i)
                        pe.wait_ge(s["hid_high"], i)
                    for f in range(FT):
                        tr = pe.transpose(HT[:, f // 4, (f % 4) * P:(f % 4 + 1) * P], hid[:, f * P:(f + 1) * P], ident[:])
                    tr.then_inc(s["hidT_done"], 1)
            emit(0, True, False, False)
            emit(1, True, True, False)
            with pe.Fori(2, NTILE - 1) as i:
                emit(i, True, True, False)
            emit(NTILE - 1, True, True, True)
            emit(NTILE, False, True, True)

        @block.scalar
        def _(act):
            act.wait_ge(s["pot_done"], 1)
            act.copy(pot_t[:], XT[0:NT].rearrange("p a b -> p (a b)")[:, 0:P]).then_inc(s["pot_ready"], 1)
            act.wait_ge(s["bias_in"], 64)
            act.copy(bias[:], raw_bias[:]).then_inc(s["split_a"], 1)
            for e in range(NE):
                act.wait_ge(load_done[e % 2], 64 * (e // 2 + 1))
                act.copy(w1h[:, e], raw_a[:, e % 2]).then_inc(s["split_a"], 1)
                act.copy(w1s[:, e], raw_b[:, e % 2]).then_inc(s["split_a"], 1)
                act.copy(w2s[:, e, :, 0:D], raw_c[:, e % 2]).then_inc(s["split_a"], 1)

            def high(i):
                act.wait_ge(s["x_turned"], i + 1)
                if not (isinstance(i, int) and i == 0):
                    act.wait_ge(s["hid_done"], i)
                act.copy(xh[:], XT[:]).then_inc(s["x_high"], 1)
            high(0)

            def emit(i, front, back_, last):
                if front:
                    act.wait_ge(s["hid_done"], i + 1)
                    if not (isinstance(i, int) and i == 0):
                        act.wait_ge(s["hidT_done"], i)
                    act.activation(hid[:].rearrange("p (n f) -> p n f", n=2), HID[:, :, 0:HALF], ACT.Gelu_apprx_tanh
                                   ).then_inc(s["hid_ready"], 1)
                    if not last:
                        high(i + 1)
                if back_:
                    act.wait_ge(s["y_done"], i)
                    act.wait_ge(s["gate_ready"], i)
                    if not isinstance(i, int) or i >= 2:
                        act.wait_ge(s["y_ready"], i - 1)
                    act.activation(low[:], Y[:, D:2 * D], ACT.Copy, scale=gate[:, 0:1]).then_inc(s["low_ready"], 1)
                if front:
                    act.wait_ge(s["hidT_done"], i + 1)
                    if not (isinstance(i, int) and i == 0):
                        act.wait_ge(s["y_done"], i)
                    act.copy(hh[:, 0:4].rearrange("p f t -> p (f t)"), HT[:, 0]).then_inc(s["idle1"], 1)
                    act.copy(hh[:, 4:6].rearrange("p f t -> p (f t)"), HT[:, 1, 0:2 * P]).then_inc(s["hid_high"], 1)
            emit(0, True, False, False)
            emit(1, True, True, False)
            with act.Fori(2, NTILE - 1) as i:
                emit(i, True, True, False)
            emit(NTILE - 1, True, True, True)
            emit(NTILE, False, True, True)

        @block.vector
        def _(dve):
            g = nc.vector
            n_step = [0]

            def then(ins):
                n_step[0] += 1
                ins.then_inc(s["step"], 1)
                dve.wait_ge(s["step"], n_step[0])
            dve.wait_ge(s["count_done"], 1)
            then(g.tensor_copy(n_of[:], MISC[:, 0:NE]))
            g.tensor_copy(n_int[:], n_of[0:1]).then_inc(s["table_ready"], 1)
            then(g.tensor_scalar(tiles_f[:], n_of[0:1], float(P - 1), None, ALU.add))
            then(g.tensor_copy(tiles_i[:], tiles_f[:]))
            then(g.tensor_scalar(tiles_i[:], tiles_i[:], 7, None, ALU.logical_shift_right))
            then(g.tensor_copy(tiles_f[:], tiles_i[:]))
            then(g.tensor_scalar(jump[:], tiles_f[:], float(-P), float(REGION), ALU.mult, ALU.add))
            then(g.memset(start[:], 0.0))
            for e in range(NE):
                then(g.tensor_tensor(start[:, e + 1:e + 2], start[:, e:e + 1], tiles_f[:, e:e + 1], ALU.add))
            dve.wait_ge(s["consts"], 5)
            then(g.memset(ex_f[:], 0.0))
            then(g.tensor_scalar(row_f[:], tile_no[:], float(P), None, ALU.mult))
            for e in range(1, NE + 1):
                if e < NE:
                    then(g.scalar_tensor_tensor(out=ex_f[:], in0=tile_no[:], scalar=start[:, e:e + 1], in1=ex_f[:],
                                                op0=ALU.is_ge, op1=ALU.add))
                then(g.tensor_scalar(past[:], tile_no[:], start[:, e:e + 1], jump[:, e - 1:e], ALU.is_ge, ALU.mult))
                then(g.tensor_tensor(row_f[:], row_f[:], past[:], ALU.add))
            then(g.tensor_scalar(row_f[:], row_f[:], float(NE * REGION), None, ALU.min))
            g.tensor_copy(ex_i[:], ex_f[:]).then_inc(s["table_ready"], 1)
            g.tensor_copy(row_i[:], row_f[:]).then_inc(s["table_ready"], 1)
            dve.wait_ge(v_in, 32)
            then(g.memset(sign[:], 1.0))
            then(g.memset(sign[:].rearrange("p (k two) -> p k two", two=2)[:, :, 1], -1.0))
            then(g.memset(chain_a[:], -1.0))
            then(g.tensor_scalar(v[:], v[:], -2.0, None, ALU.add))
            then(g.tensor_tensor(chain_a[0:32, 0:T, 0], v[0:32], sign[0:32], ALU.mult))
            then(g.tensor_tensor(chain_a[32:48, 0:T, 0], v[32:48, ::-1], sign[32:48], ALU.mult))
            g.tensor_copy(chain[:, 0], chain_a[:, 0]).then_inc(s["chain_set"], 1)
            g.tensor_copy(state[:, STEPS - 1], chain_a[:, 0]).then_inc(s["chain_set"], 1)
            dve.wait_ge(s["split_a"], 1)
            dve.wait_ge(s["bias_in"], 64)
            g.tensor_tensor(bias[32:40], raw_bias[32:40], bias[32:40].bitcast(F32), ALU.subtract).then_inc(s["dve_setup"], 1)
            for e in range(NE):
                dve.wait_ge(load_done[e % 2], 64 * (e // 2 + 1))
                dve.wait_ge(s["split_a"], 3 * e + 4)
                g.tensor_tensor(w1l[:, e], raw_a[:, e % 2], w1h[:, e].bitcast(F32), ALU.subtract).then_inc(s["split_v"], 1)
                g.tensor_tensor(w1s[EMB:P, e], raw_b[EMB:P, e % 2], w1s[EMB:P, e].bitcast(F32), ALU.subtract).then_inc(s["split_v"], 1)
                g.tensor_tensor(w2s[:, e, :, D:], raw_c[:, e % 2], w2s[:, e, :, 0:D].bitcast(F32), ALU.subtract).then_inc(s["split_v"], 1)

            def low_x(i):
                dve.wait_ge(s["x_high"], i + 1)
                if not (isinstance(i, int) and i == 0):
                    dve.wait_ge(s["hid_done"], i)
                g.tensor_tensor(xl[:], XT[:], xh[:].bitcast(F32), ALU.subtract).then_inc(s["x_low"], 1)
            low_x(0)

            def chain_step(i, m):
                n = CHAIN_OPS * (STEPS * (i - 1) + m)
                now, after = state[:, (m - 1) % STEPS], state[:, m]
                if m == 0:
                    dve.wait_ge(s["chain_kept"], 2 * i - 1)
                if m or not isinstance(i, int) or i >= 2:
                    dve.wait_ge(s["chain_step"], n)
                g.tensor_tensor_reduce(out=square[:], in0=now, in1=now, scale=1.0, scalar=0.0,
                                       op0=ALU.mult, op1=ALU.add, accum_out=size[:]).then_inc(s["chain_step"], 1)
                dve.wait_ge(s["chain_step"], n + 1)
                g.reciprocal(size[:], size[:]).then_inc(s["chain_step"], 1)
                dve.wait_ge(s["chain_step"], n + 2)
                g.scalar_tensor_tensor(out=after, in0=now, scalar=size[:, 0:1], in1=next_a[:, m],
                                       op0=ALU.mult, op1=ALU.add).then_inc(s["chain_step"], 1)

            def emit(i, front, back_, last, chained=False):
                if front and not last:
                    low_x(i + 1)
                if chained:
                    chain_step(i, 0)
                    chain_step(i, 1)
                if back_:
                    dve.wait_ge(s["low_ready"], i)
                    if not isinstance(i, int) or i >= 2:
                        dve.wait_ge(s["y_out"], 16 * (i - 1))
                    g.scalar_tensor_tensor(out=y[:], in0=Y[:, 0:D], scalar=gate[:, 0:1], in1=low[:],
                                           op0=ALU.mult, op1=ALU.add).then_inc(s["y_ready"], 1)
                if front:
                    dve.wait_ge(s["idle1"], i + 1)
                    g.tensor_tensor(hl[:, 0:4].rearrange("p f t -> p (f t)"), HT[:, 0],
                                    hh[:, 0:4].rearrange("p f t -> p (f t)").bitcast(F32), ALU.subtract).then_inc(s["idle2"], 1)
                if chained:
                    chain_step(i, 2)
                if front:
                    dve.wait_ge(s["hid_high"], i + 1)
                    g.tensor_tensor(hl[:, 4:6].rearrange("p f t -> p (f t)"), HT[:, 1, 0:2 * P],
                                    hh[:, 4:6].rearrange("p f t -> p (f t)").bitcast(F32), ALU.subtract).then_inc(s["hid_low"], 1)
                if chained:
                    chain_step(i, 3)
            emit(0, True, False, False)
            emit(1, True, True, False, chained=True)
            with dve.Fori(2, 1 + CHAIN_TILES) as i:
                emit(i, True, True, False, chained=True)
            with dve.Fori(1 + CHAIN_TILES, NTILE - 1) as i:
                emit(i, True, True, False)
            emit(NTILE - 1, True, True, True)
            emit(NTILE, False, True, True)
            dve.wait_ge(s["chain_kept"], 2 * CHAIN_TILES)
            then(g.tensor_copy(back[:], chain[32:48, 0:T][:, ::-1]))
            then(g.tensor_tensor(z[:, 0], chain[0:B, 0:T, 0], back[:, :, 0], ALU.subtract))
            then(g.tensor_tensor(z[:, 0], z[:, 0], sign[0:B], ALU.mult))
            then(g.tensor_tensor(z[:, 0], z[:, 0], v[0:B], ALU.subtract))
            then(g.scalar_tensor_tensor(out=z[:, 1], in0=chain[0:B, 0:T, 1], scalar=1.0, in1=back[:, :, 1],
                                        op0=ALU.add, op1=ALU.add))
            then(g.tensor_tensor(z2[:], z[:], z[:], ALU.mult))
            then(g.tensor_tensor(back[:, :, 0], z2[:, 0], z2[:, 1], ALU.add))
            then(g.reciprocal(back[:, :, 1], back[:, :, 0]))
            then(g.tensor_tensor(z2[:, 0], z[:, 0], back[:, :, 1], ALU.mult))
            then(g.scalar_tensor_tensor(out=z2[:, 1], in0=z[:, 1], scalar=-1.0, in1=back[:, :, 1],
                                        op0=ALU.mult, op1=ALU.mult))
            g.tensor_scalar(z2[:], z2[:], -FEAT_CLAMP, FEAT_CLAMP, ALU.max, ALU.min).then_inc(s["chain_done"], 1)


def output_block(nc, a, h2_dram, y_dram, g_dram, out):
    SLOTS = 4
    GROUPS = B // SLOTS
    with ExitStack() as ctx:
        sb = lambda n, s, d=F32: ctx.enter_context(nc.sbuf_tensor(n, s, d))
        sem = lambda n: ctx.enter_context(nc.semaphore(n))
        w_raw, scale, w = sb("o_w_raw", [3, D]), sb("o_scale", [3, D]), sb("o_w", [3, D])
        gf = [sb(f"o_gf{k}", [3, T]) for k in range(SLOTS)]
        res = [sb(f"o_res{k}", [P, TJ, D]) for k in range(SLOTS)]
        rows = [sb(f"o_rows{k}", [P, TJ, 2, D]) for k in range(SLOTS)]
        spec = [ctx.enter_context(nc.psum_tensor(f"o_spec{k}", [P, TJ, D + EMB], F32)) for k in range(SLOTS)]
        w_in, ones_ready, w_ready = sem("o_w_in"), sem("o_ones_ready"), sem("o_w_ready")
        loaded = [sem(f"o_loaded{k}") for k in range(SLOTS)]
        spec_done, half_done, sum_done = sem("o_spec_done"), sem("o_half_done"), sem("o_sum_done")
        out_done = [sem(f"o_out_done{k}") for k in range(SLOTS)]
        other_done = sem("o_other_done")
        block = ctx.enter_context(nc.Block())
        y_view = y_dram[0:2 * B * T].rearrange("(b j p k) d -> b p j (k d)", j=TJ, p=P, k=2)
        out_view = out.rearrange("b (j p) d -> b p j d", j=TJ)

        @block.sync
        def _(sp):
            sp.dma_start(w_raw[:], a["out_wb"]).then_inc(w_in, 16)
            sp.dma_start(scale[:], a["bk_scale"].broadcast_to([3, D])).then_inc(w_in, 16)
            sp.wait_ge(ones_ready, SLOTS)

            def group(n, later):
                for k in range(SLOTS):
                    b = n * SLOTS + k
                    one = lambda t: t[bass.ds(b, 1)]
                    if later:
                        sp.wait_ge(out_done[k], 16 * n)
                    sp.dma_start(res[k][:], h2_dram[:, bass.ds(b, 1)].rearrange("p b (j d) -> p (b j) d", j=TJ)
                                 ).then_inc(loaded[k], 16)
                    sp.dma_start(rows[k][:].rearrange("p j k d -> p j (k d)"),
                                 one(y_view).rearrange("b p j d -> (b p) j d")).then_inc(loaded[k], 16)
                    sp.dma_start(gf[k][0:2], g_dram[:, bass.ds(b, 1)].rearrange("c b t -> (c b) t")
                                 ).then_inc(loaded[k], 16)
            group(0, False)
            with sp.Fori(1, GROUPS) as n:
                group(n, True)

        @block.gpsimd
        def _(pool):
            for k in range(SLOTS):
                nc.gpsimd.memset(gf[k][:], 1.0).then_inc(ones_ready, 1)
            with pool.Fori(0, GROUPS) as n:
                for k in range(SLOTS):
                    pool.wait_ge(loaded[k], 48 * (n + 1))
                    nc.gpsimd.tensor_tensor(res[k][:], res[k][:], rows[k][:, :, 0], ALU.add).then_inc(half_done, 1)

        @block.tensor
        def _(pe):
            pe.wait_ge(w_ready, 1)

            def group(n, later):
                for k in range(SLOTS):
                    pe.wait_ge(loaded[k], 48 * (n + 1))
                    if later:
                        pe.wait_ge(out_done[k], 16 * n)
                    for j in range(TJ):
                        mm = pe.matmul(spec[k][:, j, 0:D], gf[k][:, j * P:(j + 1) * P], w[:], start=True, stop=True)
                    mm.then_inc(spec_done, 1)
            group(0, False)
            with pe.Fori(1, GROUPS) as n:
                group(n, True)

        @block.vector
        def _(dve):
            dve.wait_ge(w_in, 32)
            nc.vector.tensor_tensor(w[:], w_raw[:], scale[:], ALU.mult).then_inc(w_ready, 1)
            with dve.Fori(0, GROUPS) as n:
                for k in range(SLOTS):
                    c = n * SLOTS + k + 1
                    dve.wait_ge(spec_done, c)
                    nc.vector.tensor_tensor(rows[k][:, :, 1], rows[k][:, :, 1], spec[k][:, :, 0:D], ALU.add
                                            ).then_inc(other_done, 1)
                    dve.wait_ge(half_done, c)
                    dve.wait_ge(other_done, c)
                    nc.vector.tensor_tensor(res[k][:], res[k][:], rows[k][:, :, 1], ALU.add).then_inc(sum_done, 1)

        @block.scalar
        def _(act):
            with act.Fori(0, GROUPS) as n:
                for k in range(SLOTS):
                    act.wait_ge(sum_done, n * SLOTS + k + 1)
                    act.dma_start(out_view[bass.ds(n * SLOTS + k, 1)].rearrange("b p j d -> (b p) j d"), res[k][:]
                                  ).then_inc(out_done[k], 16)
            for k in range(SLOTS):
                act.wait_ge(out_done[k], 16 * GROUPS)


def vit_layer(nc, a, out):
    scratch = lambda n, shape: nc.dram_tensor(n, shape, F32).ap()
    h_dram, h2_dram = scratch("h_dram", (P, B, TJ * D)), scratch("h2_dram", (P, B, TJ * D))
    xs_dram = scratch("xs_dram", (NSLOT, ROW))
    y_dram = scratch("y_dram", (2 * B * T + P, D))
    v_dram, g_dram = scratch("v_dram", (NT, P)), scratch("g_dram", (2, B, T))
    with ExitStack() as ctx:
        sb = lambda n, s: ctx.enter_context(nc.sbuf_tensor(n, s, F32))
        ident = sb("ident", [P, P])
        count = sb("count", [P, NE])
        pot = sb("pot", [P, B, TJ])
        keep = dict(ident=ident, count=count, pot=pot)
        tokens_block(nc, a, ident, h_dram)
        attention_block(nc, a, keep, h_dram, h2_dram, xs_dram)
        experts_block(nc, a, keep, xs_dram, y_dram, v_dram, g_dram)
        output_block(nc, a, h2_dram, y_dram, g_dram, out)


def layouts(i):
    c = np.ascontiguousarray
    x = i["x"]
    o = {}
    for n, p in enumerate((1, 2, 4)):
        g = 64 // p
        o[f"x{n}"] = c(x.reshape(B, 3, g, p, g, p).transpose(2, 4, 0, 3, 5, 1).reshape(g * g, B * p * p * 3))
    o["idx"] = c(np.concatenate([i["L0_tok_idx0"].reshape(2, P, 16).transpose(1, 0, 2).reshape(P, 32),
                                 i["L0_tok_idx1"].reshape(64, 2, 8).transpose(1, 0, 2).reshape(P, 8),
                                 i["L0_tok_idx2"].reshape(16, 8, 2).transpose(1, 0, 2).reshape(P, 2)], 1))
    o["w0"] = c(i["L0_tok_W0"].T)
    o["w1"] = c(i["L0_tok_W1"].T.reshape(2, KH, EMB).transpose(1, 0, 2))
    o["w2"] = c(i["L0_tok_W2"].T.reshape(16, 48, EMB).transpose(1, 0, 2))
    o["tok_b"] = c(np.stack([i[f"L0_tok_b{n}"] for n in range(3)], 1))
    o["wf"] = c(i["L0_tok_Wf"].T)
    o["bf"] = i["L0_tok_bf"].reshape(1, D)
    o["up1"] = upsampling(64)
    o["up2"] = np.concatenate([upsampling(16), np.ones((1, T), np.float32)])
    w, b = i["L0_attn_w_inp"][0], i["L0_attn_b_inp"]
    o["wqk_t"] = c(np.concatenate([w.T, b[:, None]], 1)[:2 * D].reshape(4, KH, D + 1).transpose(1, 0, 2))

    def halves(w, b):
        n = w.shape[1]
        return np.concatenate([w.reshape(2, KH, n).transpose(1, 0, 2), np.broadcast_to(b, (1, 2, n))], 0)
    o["wv"] = halves(w[:, 2 * D:], b[2 * D:])
    o["w_out"] = halves(i["L0_attn_w_out"][0], i["L0_attn_b_out"])
    o["w_gate"] = halves(np.concatenate([i["L0_ffn_gate_w"], i["L0_ffn_v_w"][:, None]], 1),
                         np.append(i["L0_ffn_gate_b"], i["L0_ffn_v_b"]))
    o["omega_t"] = c(i["L0_attn_omega"].T)
    for n in ("w1", "b1", "w2", "b2"):
        o["e" + n] = i["L0_ffn_" + n]
    o["out_wb"] = np.concatenate([i["L0_ffn_out_w"], i["L0_ffn_out_b"][None]])
    o["bk_scale"] = i["L0_ffn_bk_scale"].reshape(1, D)
    return {n: c(v) for n, v in o.items()}


def kernel(**inputs):
    import concourse.bacc as bacc
    from concourse.bass_utils import run_bass_kernel_spmd

    nc = bacc.Bacc("TRN2", target_bir_lowering=False, num_devices=1)
    arrays = layouts({n: np.asarray(v) for n, v in inputs.items()})
    a = {n: nc.dram_tensor("in_" + n, v.shape, mybir.dt.from_np(v.dtype), kind="ExternalInput").ap()
         for n, v in arrays.items()}
    out = nc.dram_tensor("result", (B, T, D), F32, kind="ExternalOutput").ap()
    vit_layer(nc, a, out)
    r = run_bass_kernel_spmd(nc, [{"in_" + n: v for n, v in arrays.items()}], core_ids=[0])
    return r.results[0]["result"]
```

```python
from contextlib import ExitStack

import numpy as np

import concourse.bass as bass
from concourse import mybir

F32, F32R, BF16 = mybir.dt.float32, mybir.dt.float32r, mybir.dt.bfloat16
U32, I32 = mybir.dt.uint32, mybir.dt.int32
ALU = mybir.AluOpType
ACT = mybir.ActivationFunctionType
AX = mybir.AxisListType.X

P = 128
B, T, D = 16, 256, 192
NT = B * T // P
TJ = T // P
KH = D // 2
EMB = 64
H, DH, NF = 12, 16, 16
HW = NF + 1
VW = DH + 1
GH = 4
NG = H // GH
NE, FF = 8, 768
REGION = B * T + P
NSLOT = NE * REGION + P
XW = D + EMB
ROW = XW + 2
NTILE = 2 * B * T // P + NE - 1
EPS_F, EPS_LN = 1e-6, 1e-5
UNITS = B
UF = NE * FF // UNITS
UT = UF // P
V_MAX, FEAT_CLAMP = 3.0, 10.0


def upsampling(n_in):
    pos = (np.arange(T, dtype=np.float32) + np.float32(0.5)) * np.float32(n_in / T) - np.float32(0.5)
    pos = np.clip(pos, 0.0, n_in - 1).astype(np.float32)
    i0 = np.floor(pos).astype(np.int32)
    i1 = np.minimum(i0 + 1, n_in - 1)
    w = (pos - i0).astype(np.float32)
    a = np.zeros((n_in, T), np.float32)
    np.add.at(a, (i0, np.arange(T)), np.float32(1) - w)
    np.add.at(a, (i1, np.arange(T)), w)
    return a


def wait_apart(eng, sem, value):
    eng.wait_ge(sem, value)
    eng.nop(nofuse=True)


def tokens_block(nc, a, ident, h_dram):
    with ExitStack() as ctx:
        sb = lambda n, s, d=F32: ctx.enter_context(nc.sbuf_tensor("t_" + n, s, d))
        sem = lambda n: ctx.enter_context(nc.semaphore(n))
        idx = sb("idx", [P, 42], U32)
        g0 = sb("g0", [P, 2, 16, 48])
        g1 = sb("g1", [P, 8, B, 12])
        g2 = sb("g2", [P, 2, B, 48])
        r0 = sb("r0", [P, 2, B, 16, 3])
        r1 = sb("r1", [P, B, 8, 12])
        t0 = sb("t0", [48, B, 2, P])
        t1 = sb("t1", [96, B, 2, 64])
        t2 = sb("t2", [48, B, 2, P])
        w0 = sb("w0", [48, EMB])
        w1 = sb("w1", [96, 2, EMB])
        w2 = sb("w2", [48, 16, EMB])
        bias = sb("bias", [EMB, 3])
        fine = sb("fine", [P, B, T])
        mix = sb("mix", [P, B, D])
        up2 = sb("up2", [17, T])
        mix2 = sb("mix2", [17, B, D])
        o1 = sb("o1", [EMB, B * 64])
        o2 = sb("o2", [EMB, B * 16])
        wf1 = sb("wf1", [EMB, D])
        wf2 = sb("wf2", [EMB, D])
        hs = sb("hs", [P, B, TJ, D])
        bank = [ctx.enter_context(nc.psum_tensor(f"tk{i}", [P, 512], F32)) for i in range(8)]

        idx_in, params_in = sem("idx_in"), sem("params_in")
        got0, got1, got2 = sem("got0"), sem("got1"), sem("got2")
        const_ready = sem("ident_ready")
        regrouped0, regrouped1 = sem("regrouped0"), sem("regrouped1")
        group_done, group_out = sem("group_done"), [sem("group_out_v"), sem("group_out_a")]
        h_out = sem("h_out")
        block = ctx.enter_context(nc.Block())

        groups = [("t2", k) for k in range(8)] + [("t1", k) for k in range(4)] + [("t0", k) for k in range(8)]
        groups = groups[:12] + [("p2", 0), ("p1", 0), ("p1", 1)] + groups[12:] + \
            [("z1", b) for b in range(B)] + [("z2", b) for b in range(B)] + \
            [("p0", k) for k in range(8)] + [("h", b) for b in range(B)]
        number = {g: n for n, g in enumerate(groups)}

        def wait_out(eng, *which):
            for par in range(2):
                n = [number[g] for g in which if number[g] % 2 == par]
                if n:
                    eng.wait_ge(group_out[par], max(n) // 2 + 1)

        @block.sync
        def _(sp):
            sp.dma_start(idx[:], a["idx"].bitcast(U32)).then_inc(idx_in, 16)
            for dst, src in ((w2[:], a["w2"]), (w1[:], a["w1"]), (w0[:], a["w0"]), (bias[:], a["tok_b"]),
                             (wf1[:], a["wf"][EMB:2 * EMB]), (wf2[:], a["wf"][2 * EMB:]), (up2[:], a["up2"]),
                             (mix[0:EMB], a["wf"][0:EMB].unsqueeze(1).broadcast_to([EMB, B, D])),
                             (mix2[16:17], a["bf"].unsqueeze(1).broadcast_to([1, B, D])),
                             (fine[EMB:P], a["up1"].unsqueeze(1).broadcast_to([64, B, T]))):
                sp.dma_start(dst, src).then_inc(params_in, 16)
            for b in range(0, B, 4):
                wait_out(sp, ("h", b + 2), ("h", b + 3))
                sp.dma_start(h_dram[:, b:b + 4], hs[:, b:b + 4].rearrange("p b j d -> p b (j d)")).then_inc(h_out, 16)
            sp.wait_ge(h_out, 16 * (B // 4))

        @block.gpsimd
        def _(pool):
            nc.gpsimd.memset(ident[:], 0.0).then_inc(const_ready, 1)
            pool.wait_ge(const_ready, 1)
            nc.gpsimd.affine_select(out=ident[:], in_=ident[:], compare_op=ALU.not_equal, fill=1.0, base=0,
                                    pattern=[[-1, P]], channel_multiplier=1).then_inc(const_ready, 1)
            pool.wait_ge(idx_in, 16)

            def gather(out, src, col, done):
                pool.indirect_dma_start(out=out, out_offset=None, in_=src,
                                        in_offset=bass.IndirectOffsetOnAxis(ap=idx[:, col:col + 1], axis=0)
                                        ).then_inc(done, 16)
            for j in range(2):
                gather(g2[:, j].rearrange("p b q -> p (b q)"), a["x2"], 40 + j, got2)
            for j in range(8):
                gather(g1[:, j].rearrange("p b q -> p (b q)"), a["x1"], 32 + j, got1)
            for t in range(2):
                for j in range(16):
                    gather(g0[:, t, j], a["x0"], t * 16 + j, got0)

        @block.tensor
        def _(pe):
            pe.wait_ge(const_ready, 2)
            for n, (what, k) in enumerate(groups):
                ps = bank[n % 8]
                if n >= 8:
                    pe.wait_ge(group_out[n % 2], (n - 8) // 2 + 1)
                if what == "t2":
                    if k == 0:
                        pe.wait_ge(got2, 32)
                    for m in range(4):
                        b, j = (4 * k + m) // 2, m % 2
                        last = pe.transpose(ps[0:48, m * P:(m + 1) * P], g2[:, j, b], ident[:])
                elif what == "t1":
                    if k == 0:
                        pe.wait_ge(regrouped1, 1)
                    for m in range(4):
                        last = pe.transpose(ps[0:96, m * P:(m + 1) * P], r1[:, 4 * k + m].rearrange("p j q -> p (j q)"), ident[:])
                elif what == "t0":
                    if k == 0:
                        pe.wait_ge(regrouped0, 2)
                    for m in range(4):
                        b, t = (4 * k + m) // 2, m % 2
                        last = pe.transpose(ps[0:48, m * P:(m + 1) * P], r0[:, t, b].rearrange("p j c -> p (j c)"), ident[:])
                elif what == "p2":
                    wait_out(pe, ("t2", 6), ("t2", 7))
                    pe.wait_ge(params_in, 160)
                    v = t2[:].rearrange("q b j (e t) -> q j e b t", e=8)
                    for j in range(16):
                        last = pe.matmul(ps[0:EMB, 0:T], w2[:, j], v[:, j % 2, j // 2], start=j == 0, stop=j == 15)
                elif what == "p1":
                    wait_out(pe, ("t1", 2), ("t1", 3))
                    for j in range(2):
                        last = pe.matmul(ps[0:EMB, :], w1[:, j], t1[:, 8 * k:8 * k + 8, j], start=j == 0, stop=j == 1)
                elif what == "p0":
                    if k == 0:
                        wait_out(pe, ("t0", 6), ("t0", 7))
                    last = pe.matmul(ps[0:EMB, :], w0[:], t0[:, 2 * k:2 * k + 2].rearrange("q b t p -> q (b t p)"),
                                     start=True, stop=True)
                elif what == "z1":
                    if k == 0:
                        wait_out(pe, ("p1", 0), ("p1", 1))
                    last = pe.matmul(ps[EMB:P, 0:D], o1[:, k * 64:(k + 1) * 64], wf1[:], start=True, stop=True)
                elif what == "z2":
                    if k == 0:
                        wait_out(pe, ("p2", 0))
                    last = pe.matmul(ps[0:16, 0:D], o2[:, k * 16:(k + 1) * 16], wf2[:], start=True, stop=True)
                else:
                    wait_out(pe, ("p0", k // 2), ("z1", k), ("z2", k))
                    for j in range(TJ):
                        tok = slice(j * P, (j + 1) * P)
                        pe.matmul(ps[:, j * D:(j + 1) * D], fine[:, k, tok], mix[:, k], start=True, stop=False)
                        last = pe.matmul(ps[:, j * D:(j + 1) * D], up2[:, tok], mix2[:, k], start=False, stop=True)
                last.then_inc(group_done, 1)

        def copy_out(eng, par, copy, add_bias):
            for n, (what, k) in enumerate(groups):
                if n % 2 != par:
                    continue
                ps = bank[n % 8]
                if what == "t2" and k == 6 + par and par == 0:
                    eng.wait_ge(got1, 16 * 8)
                    copy(r1[:], g1[:].rearrange("p j b q -> p b j q")).then_inc(regrouped1, 1)
                if (what, k) in (("p1", 0), ("p1", 1)):
                    eng.wait_ge(got0, 16 * 32)
                    copy(r0[:, par], g0[:, par].rearrange("p j (b c) -> p b j c", c=3)).then_inc(regrouped0, 1)
                eng.wait_ge(group_done, n + 1)
                if what == "t2":
                    ins = copy(t2[:, 2 * k:2 * k + 2].rearrange("q b j p -> q (b j p)"), ps[0:48, :])
                elif what == "t1":
                    ins = copy(t1[:, 4 * k:4 * k + 4].rearrange("q b j p -> q (b j p)"), ps[0:96, :])
                elif what == "t0":
                    ins = copy(t0[:, 2 * k:2 * k + 2].rearrange("q b j p -> q (b j p)"), ps[0:48, :])
                elif what == "p2":
                    eng.wait_ge(params_in, 160)
                    ins = add_bias(o2[:], ps[0:EMB, 0:T], bias[:, 2:3])
                elif what == "p1":
                    eng.wait_ge(params_in, 160)
                    ins = add_bias(o1[:, k * 512:(k + 1) * 512], ps[0:EMB, :], bias[:, 1:2])
                elif what == "p0":
                    ins = add_bias(fine[0:EMB, 2 * k:2 * k + 2].rearrange("e b t -> e (b t)"), ps[0:EMB, :], bias[:, 0:1])
                elif what == "z1":
                    ins = copy(mix[EMB:P, k], ps[EMB:P, 0:D])
                elif what == "z2":
                    ins = copy(mix2[0:16, k], ps[0:16, 0:D])
                else:
                    ins = copy(hs[:, k].rearrange("p j d -> p (j d)"), ps[:, 0:TJ * D])
                ins.then_inc(group_out[par], 1)

        @block.vector
        def _(dve):
            copy_out(dve, 0, lambda o, i: dve.tensor_copy(o, i),
                     lambda o, i, s: dve.tensor_scalar(o, i, s, None, ALU.add))

        @block.scalar
        def _(act):
            copy_out(act, 1, lambda o, i: act.copy(o, i),
                     lambda o, i, s: act.activation(o, i, ACT.Identity, bias=s))


def expert_weights(nc, ctx):
    w = {n: ctx.enter_context(nc.sbuf_tensor("x_" + n, [P, UNITS, UF], F32R)) for n in ("w1h", "w1l")}
    w["w2s"] = ctx.enter_context(nc.sbuf_tensor("x_w2s", [P, UNITS, UT, 2 * D], F32R))
    return w


def attention_block(nc, a, keep, h_dram, h2_dram, xs_dram):
    ident, count, pot = keep["ident"], keep["count"], keep["pot"]
    w1h, w1l, w2s = (keep[n] for n in ("w1h", "w1l", "w2s"))
    with ExitStack() as ctx:
        sb = lambda n, s, d=F32: ctx.enter_context(nc.sbuf_tensor("a_" + n, s, d))
        raw_a, raw_c = sb("raw_a", [P, UF]), sb("raw_c", [P, UT, D])
        ps = lambda n, s: ctx.enter_context(nc.psum_tensor("a_" + n, s, F32))
        sem = lambda n: ctx.enter_context(nc.semaphore(n))
        causal = sb("causal", [P, P])
        before = sb("before", [P, P], BF16)
        ones = sb("ones", [P, P], BF16)
        block_mask = sb("block_mask", [P, GH, VW])
        eps_col = sb("eps_col", [P, 1])
        first = sb("first", [P, NE])
        region = sb("region", [P, NE])
        omega = sb("omega", [KH, H // 2, HW])
        wqk_t = sb("wqk_t", [KH, 4, D + 1])
        wqkv = sb("wqkv", [KH + 1, 2, 2 * H * HW + D])
        w_out = sb("w_out", [KH + 1, 2, D])
        w_gate = sb("w_gate", [KH + 1, 2, NE + 1])
        hb = sb("hb", [P, 4, TJ, D])
        stats, mv, rstd1 = sb("stats", [P, TJ, 6]), sb("mv", [P, TJ, 2]), sb("rstd1", [P, TJ])
        var_eps = {n: sb("var_eps_" + n, [P, TJ]) for n in ("rstd1_ready", "rstd2_ready")}
        minus_half = sb("minus_half", [P, TJ])
        xn = sb("xn", [P, TJ, D])
        xn_t = sb("xn_t", [KH + 1, 2, T])
        top = sb("top", [P, 2 * H])
        top_k = sb("top_k", [P, 1])
        shift = sb("shift", [P, 2 * H])
        feat = [sb(f"feat{j}", [P, 2 * H, 32]) for j in range(TJ)]
        kf = sb("kf", [P, H, 32])
        values = sb("values", [P, 2, TJ, H, VW])
        qb_t = sb("qb_t", [P, NG, TJ, GH, P])
        qf_t, kf_t = sb("qf_t", [P, NG, P]), sb("kf_t", [P, NG, T])
        state = sb("state", [P, NG, GH * VW])
        masked = [sb(f"masked{i}", [P, GH, P]) for i in range(2)]
        den = sb("den", [P, TJ * H])
        att = sb("att", [P, TJ, D])
        att_t = sb("att_t", [KH + 1, 2, T])
        h2 = sb("h2", [P, 2, TJ, D])
        stats2, mv2, rstd2 = sb("stats2", [P, TJ, 6]), sb("mv2", [P, TJ, 2]), sb("rstd2", [P, TJ])
        xn2 = sb("xn2", [P, TJ, D])
        xn2_t = sb("xn2_t", [KH + 1, 2, T])
        logits = sb("logits", [P, TJ, NE])
        prob, eq, w8 = sb("prob", [P, TJ, NE]), sb("eq", [P, TJ, NE]), sb("w8", [P, TJ, NE])
        pick = [sb(f"pick{k}", [P, TJ, NE]) for k in range(2)]
        m = sb("m", [P, 6, TJ])
        gate = sb("gate", [P, TJ, 2])
        chosen = sb("chosen", [P, TJ, NE], BF16)
        earlier = sb("earlier", [P, TJ, NE], BF16)
        slot_e, slot_f = sb("slot_e", [P, TJ, NE]), sb("slot_f", [P, TJ, 2])
        slot = sb("slot", [P, TJ, 2], U32)
        dest = sb("dest", [P, TJ, 2])
        rows = sb("rows", [P, TJ, 2, ROW])
        R = [ps(f"r{i}", [P, 512]) for i in range(4)]
        S = [ps(f"s{i}", [P, GH, P]) for i in range(2)]
        AB = ps("ab", [P, 512])
        M = ps("misc", [P, 512])

        names = """w_in setup pool_const h_in xn_ready xnT_done xnT_out qk_done v_done v_out top_done shift_done
            feat_ready kf_ready qT_done qT_out state_done state_out s_done s_out av_done att_ready attT_done
            attT_out proj_done h2_ready xn2_ready xn2T_done xn2T_out logit_done logit_out logit_max prob_ready
            chosen_ready slots_ready prefix_done rows_ready scattered h2_stored dve_step
            w_done gated tail rows_x rstd1_ready rstd2_ready gate_step count_step place_step norm_step att_step raw_in high low""".split()
        s = {n: sem("b_" + n) for n in names}
        block = ctx.enter_context(nc.Block())
        NSETUP = 15

        def sched(eng, emit):
            emit(0, True, False, False, False)
            emit(1, True, True, False, False)
            emit(2, True, True, True, False)
            emit(3, True, True, True, True)
            with eng.Fori(4, B - 1) as i:
                emit(i, True, True, True, True)
            emit(B - 1, True, True, True, True)
            emit(B, False, True, True, True)
            emit(B + 1, False, False, True, True)
            emit(B + 2, False, False, False, True)

        @block.sync
        def _(sp):
            loads = [(omega[h * NF:(h + 1) * NF, h, 0:NF], a["omega_t"]) for h in range(6)]
            loads += [(wqk_t[:], a["wqk_t"]), (wqkv[:, :, 2 * H * HW:], a["wv"]), (w_out[:], a["w_out"]),
                      (w_gate[:], a["w_gate"]), ]
            sp.wait_ge(s["pool_const"], 1)
            for dst, src in loads:
                sp.dma_start(dst, src).then_inc(s["w_in"], 16)

            def load_h(b):
                sp.dma_start(hb[:, b % 4], h_dram[:, bass.ds(b, 1)].rearrange("p b (j d) -> p (b j) d", j=TJ)
                             ).then_inc(s["h_in"], 16)

            def emit(i, one, two, tail, choice):
                if one:
                    if not (isinstance(i, int) and i == 0):
                        wait_apart(sp, s["low"], 2 * i)
                    cut = lambda t: t[:, bass.ds(i, 1)].rearrange("k u f -> k (u f)")
                    sp.dma_start(raw_a[:], cut(a["ew1"][0:P])).then_inc(s["raw_in"], 16)
                    sp.dma_start(raw_c[:], a["ew2"][:, bass.ds(i, 1)].rearrange("k u f d -> k (u f) d")
                                 ).then_inc(s["raw_in"], 16)
                if one and not (isinstance(i, int) and i == B - 1):
                    if not isinstance(i, int) or i >= 3:
                        sp.wait_ge(s["h2_ready"], i - 2)
                    sp.wait_ge(s["h_in"], 16 * (i + 1))
                    load_h(i + 1)
                if tail:
                    wait_apart(sp, s["h2_ready"], i - 1)
                    if not isinstance(i, int) or i >= 3:
                        wait_apart(sp, s["h2_stored"], 16 * (i - 2))
                    sp.dma_start(h2_dram[:, bass.ds(i - 2, 1)].rearrange("p b (j d) -> p (b j) d", j=TJ),
                                 h2[:, i % 2]).then_inc(s["h2_stored"], 16)
            load_h(0)
            sched(sp, emit)
            sp.wait_ge(s["h2_stored"], 16 * B)

        @block.gpsimd
        def _(pool):
            g = nc.gpsimd
            g.memset(omega[:], 0.0).then_inc(s["pool_const"], 1)
            g.memset(causal[:], 1.0).then_inc(s["setup"], 1)
            g.memset(before[:], 1.0).then_inc(s["setup"], 1)
            g.memset(ones[:], 1.0).then_inc(s["setup"], 1)
            g.memset(block_mask[:], 1.0).then_inc(s["setup"], 1)
            g.memset(qb_t[:], 0.0).then_inc(s["setup"], 1)
            g.iota(first[:], [[-1, NE]], base=NE, channel_multiplier=0,
                   allow_small_or_imprecise_dtypes=True).then_inc(s["setup"], 1)
            g.iota(region[:], [[REGION, NE]], base=0, channel_multiplier=0,
                   allow_small_or_imprecise_dtypes=True).then_inc(s["setup"], 1)
            g.iota(dest[:], [[2 * P, TJ], [1, 2]], base=0, channel_multiplier=2,
                   allow_small_or_imprecise_dtypes=True).then_inc(s["setup"], 1)
            g.memset(xn_t[:], 1.0).then_inc(s["setup"], 1)
            g.memset(att_t[:], 1.0).then_inc(s["setup"], 1)
            g.memset(xn2_t[:], 1.0).then_inc(s["setup"], 1)
            g.memset(feat[0][:], 0.0).then_inc(s["setup"], 1)
            g.memset(feat[1][:], 0.0).then_inc(s["setup"], 1)
            g.memset(values[:], 1.0).then_inc(s["setup"], 1)
            g.memset(minus_half[:], -0.5).then_inc(s["setup"], 1)
            pool.wait_ge(s["setup"], NSETUP)
            g.affine_select(out=causal[:], in_=causal[:], compare_op=ALU.is_ge, fill=0.0, base=0,
                            pattern=[[1, P]], channel_multiplier=-1).then_inc(s["setup"], 1)
            g.affine_select(out=before[:], in_=before[:], compare_op=ALU.is_gt, fill=0.0, base=0,
                            pattern=[[1, P]], channel_multiplier=-1).then_inc(s["setup"], 1)
            g.affine_select(out=block_mask[:], in_=block_mask[:], compare_op=ALU.is_ge, fill=0.0, base=0,
                            pattern=[[-32, GH], [0, VW]], channel_multiplier=1).then_inc(s["setup"], 1)
            pool.wait_ge(s["setup"], NSETUP + 3)
            g.affine_select(out=block_mask[:], in_=block_mask[:], compare_op=ALU.is_gt, fill=0.0, base=NF,
                            pattern=[[32, GH], [0, VW]], channel_multiplier=-1).then_inc(s["setup"], 1)

            def rstd(ready, b, mv, out, sem_name, count):
                wait_apart(pool, s[sem_name], count)
                g.tensor_scalar(var_eps[ready][:], mv[:, :, 1], EPS_LN, None, ALU.add).then_inc(s[ready], 1)
                pool.wait_ge(s[ready], 2 * b + 1)
                g.tensor_tensor(out[:], var_eps[ready][:], minus_half[:], ALU.pow).then_inc(s[ready], 1)

            rstd("rstd1_ready", 0, mv, rstd1, "norm_step", 4)

            def emit(i, one, two, tail, choice):
                if one and not (isinstance(i, int) and i == B - 1):
                    rstd("rstd1_ready", i + 1, mv, rstd1, "norm_step", 5 * (i + 1) + 4)
                if one:
                    wait_apart(pool, s["high"], 2 * (i + 1))
                    u = lambda t: t[:, bass.ds(i, 1)].rearrange("k u f -> k (u f)")
                    v = lambda t, c: t[:, bass.ds(i, 1), :, c].rearrange("k u f d -> k (u f) d")
                    g.tensor_tensor(u(w1l), raw_a[:], u(w1h).bitcast(F32), ALU.subtract).then_inc(s["low"], 1)
                    g.tensor_tensor(v(w2s, slice(D, 2 * D)), raw_c[:], v(w2s, slice(0, D)).bitcast(F32), ALU.subtract
                                    ).then_inc(s["low"], 1)
                if one:
                    if not (isinstance(i, int) and i == 0):
                        pool.wait_ge(s["state_done"], i)
                    wait_apart(pool, s["feat_ready"], TJ * i + 1)
                    g.tensor_scalar(kf[:], feat[0][:, H:2 * H], EPS_F, None, ALU.add).then_inc(s["kf_ready"], 1)
                if tail:
                    rstd("rstd2_ready", i - 2, mv2, rstd2, "tail", 5 * (i - 2) + 4)
                if choice:
                    if not isinstance(i, int) or i >= 4:
                        pool.wait_ge(s["scattered"], 64 * (i - 3))
                    pool.wait_ge(s["rows_ready"], 2 * (i - 2))
                    wait_apart(pool, s["rows_x"], 4 * (i - 2))
                    for j in range(TJ):
                        for k in range(2):
                            pool.indirect_dma_start(
                                out=xs_dram, in_=rows[:, j, k], in_offset=None,
                                out_offset=bass.IndirectOffsetOnAxis(ap=slot[:, j, k:k + 1], axis=0)
                            ).then_inc(s["scattered"], 16)
            sched(pool, emit)
            pool.wait_ge(s["scattered"], 16 * 4 * B)

        @block.tensor
        def _(pe):
            pe.wait_ge(s["w_in"], 160)
            pe.wait_ge(s["dve_step"], 2)
            for half, rows_n in ((0, KH), (1, KH + 1)):
                for n in range(4):
                    last = pe.matmul(R[half][0:rows_n, n * 6 * HW:(n + 1) * 6 * HW],
                                     wqk_t[:, n, half * KH:half * KH + rows_n],
                                     omega[:].rearrange("d h f -> d (h f)"), start=True, stop=True)
            last.then_inc(s["w_done"], 1)
            pe.wait_ge(s["gated"], 2)
            pe.wait_ge(s["setup"], NSETUP + 4)

            def turn(dst, src, n=KH):
                for c in range(2):
                    for j in range(TJ):
                        last = pe.transpose(dst[0:KH, c * T + j * P:c * T + (j + 1) * P],
                                            src[:, j, c * KH:(c + 1) * KH], ident[:])
                return last

            def emit(i, one, two, tail, choice):
                start0 = isinstance(i, int) and i == 0
                b = i - 1

                def scores(g):
                    for j in range(TJ):
                        n = 2 * g + j
                        if not (isinstance(i, int) and i == 1) or n >= 2:
                            pe.wait_ge(s["s_out"], 6 * b + n - 1)
                        pe.matmul(S[j][:].rearrange("p h t -> p (h t)"), kf_t[:, g, j * P:(j + 1) * P],
                                  qb_t[:, g, j].rearrange("p h t -> p (h t)"), start=True, stop=True
                                  ).then_inc(s["s_done"], 1)

                def averages(g):
                    for j in range(TJ):
                        o = j * H * VW + g * GH * VW
                        if j == 1:
                            pe.matmul(AB[:, o:o + GH * VW], qf_t[:, g], state[:, g],
                                      start=True, stop=False, skip_group_check=True)
                        pe.wait_ge(s["s_out"], 6 * b + 2 * g + j + 1)
                        for r in range(GH):
                            last = pe.matmul(AB[:, o + r * VW:o + (r + 1) * VW], masked[j][:, r],
                                             values[:, (i + 1) % 2, j, g * GH + r], start=j == 0, stop=True,
                                             skip_group_check=True)
                        last.then_inc(s["av_done"], 1)

                def qk(j):
                    for c in range(2):
                        last = pe.matmul(R[2 + j][:, 0:2 * H * HW], xn_t[0:KH + c, c, j * P:(j + 1) * P],
                                         wqkv[0:KH + c, c, 0:2 * H * HW], start=c == 0, stop=c == 1)
                    last.then_inc(s["qk_done"], 1)

                def project_values(j):
                    for c in range(2):
                        last = pe.matmul(R[1][:, j * D:(j + 1) * D], xn_t[0:KH + c, c, j * P:(j + 1) * P],
                                         wqkv[0:KH + c, c, 2 * H * HW:], start=c == 0, stop=c == 1)
                    if j == 1:
                        last.then_inc(s["v_done"], 1)

                def turn_features(j, banks):
                    pe.wait_ge(s["feat_ready"], TJ * i + j + 1)
                    for n in range(2):
                        for g in range(NG):
                            last = pe.transpose(R[banks[n]][:, g * P:(g + 1) * P],
                                                feat[j][:, n * H + g * GH:n * H + (g + 1) * GH].rearrange("p h f -> p (h f)"),
                                                ident[:])
                        last.then_inc(s["qT_done"], 1)

                if two:
                    pe.wait_ge(s["kf_ready"], i)
                    pe.wait_ge(s["v_out"], i)
                    if not isinstance(i, int) or i >= 4:
                        pe.wait_ge(s["slots_ready"], i - 3)
                    for g in range(NG):
                        last = pe.matmul(M[:, g * GH * VW:(g + 1) * GH * VW],
                                         kf[:, g * GH:(g + 1) * GH].rearrange("p h f -> p (h f)"),
                                         values[:, (i + 1) % 2, 0, g * GH:(g + 1) * GH].rearrange("p h v -> p (h v)"),
                                         start=True, stop=True)
                    last.then_inc(s["state_done"], 1)
                if tail:
                    pe.wait_ge(s["att_ready"], i - 1)
                    pe.wait_ge(s["qT_out"], min(4 * i, 4 * B) - 2 if isinstance(i, int) else 4 * i - 2)
                    turn(R[1], att).then_inc(s["attT_done"], 1)
                if one:
                    pe.wait_ge(s["xn_ready"], i + 1)
                    if not start0:
                        pe.wait_ge(s["qT_out"], 4 * i)
                    turn(R[0], xn).then_inc(s["xnT_done"], 1)
                if two:
                    pe.wait_ge(s["qT_out"], 4 * i)
                    scores(0)
                if one:
                    pe.wait_ge(s["xnT_out"], i + 1)
                    qk(0)
                if two:
                    pe.wait_ge(s["state_out"], i)
                    if not isinstance(i, int) or i >= 2:
                        pe.wait_ge(s["att_ready"], i - 1)
                    averages(0)
                if tail:
                    pe.wait_ge(s["attT_out"], i - 1)
                    if not one:
                        pe.wait_ge(s["qT_out"], 4 * B)
                    for j in range(TJ):
                        for c in range(2):
                            last = pe.matmul(R[0][:, j * D:(j + 1) * D], att_t[0:KH + c, c, j * P:(j + 1) * P],
                                             w_out[0:KH + c, c], start=c == 0, stop=c == 1)
                    last.then_inc(s["proj_done"], 1)
                if two:
                    scores(1)
                if one:
                    if not isinstance(i, int) or i >= 3:
                        pe.wait_ge(s["logit_out"], i - 2)
                    qk(1)
                    project_values(0)
                    project_values(1)
                if two:
                    averages(1)
                    scores(2)
                if one:
                    if tail:
                        pe.wait_ge(s["h2_ready"], i - 1)
                    pe.wait_ge(s["v_out"], i + 1)
                    turn_features(0, (0, 1))
                if tail:
                    pe.wait_ge(s["xn2_ready"], i - 1)
                    if one:
                        pe.wait_ge(s["shift_done"], TJ * i + 1)
                    turn(R[2], xn2).then_inc(s["xn2T_done"], 1)
                if two:
                    averages(2)
                if one:
                    pe.wait_ge(s["shift_done"], TJ * i + 2)
                    if tail:
                        pe.wait_ge(s["xn2T_out"], i - 1)
                    pe.wait_ge(s["qT_out"], 4 * i + 1)
                    turn_features(1, (2, 0))
                if choice:
                    pe.wait_ge(s["chosen_ready"], i - 2)
                    if two:
                        pe.wait_ge(s["state_out"], i)
                    pe.matmul(M[:, 0:TJ * NE], before[:], chosen[:].rearrange("p j e -> p (j e)"), start=True, stop=False)
                    pe.matmul(M[:, 0:TJ * NE], ones[:], earlier[:].rearrange("p j e -> p (j e)"), start=False, stop=True
                              ).then_inc(s["prefix_done"], 1)
                if tail:
                    pe.wait_ge(s["xn2T_out"], i - 1)
                    for j in range(TJ):
                        for c in range(2):
                            last = pe.matmul(R[3][:, j * (NE + 1):(j + 1) * (NE + 1)],
                                             xn2_t[0:KH + c, c, j * P:(j + 1) * P], w_gate[0:KH + c, c],
                                             start=c == 0, stop=c == 1)
                    last.then_inc(s["logit_done"], 1)
            sched(pe, emit)

        @block.scalar
        def _(act):
            act.wait_ge(s["w_done"], 1)
            for half, n in ((0, KH), (1, KH + 1)):
                act.mul(wqkv[0:n, half, 0:2 * H * HW], R[half][0:n, 0:2 * H * HW], float(DH) ** -0.25
                        ).then_inc(s["gated"], 1)
            act.wait_ge(s["setup"], NSETUP + 4)
            act.wait_ge(s["dve_step"], 5)

            def emit(i, one, two, tail, choice):
                if choice:
                    act.wait_ge(s["logit_max"], i - 2)
                    act.activation(prob[:], logits[:], ACT.Exp).then_inc(s["prob_ready"], 1)
                if tail:
                    act.wait_ge(s["attT_done"], i - 1)
                    act.copy(att_t[0:KH].rearrange("d c t -> d (c t)"), R[1][0:KH, 0:2 * T]).then_inc(s["attT_out"], 1)
                if one:
                    act.wait_ge(s["xnT_done"], i + 1)
                    act.copy(xn_t[0:KH].rearrange("d c t -> d (c t)"), R[0][0:KH, 0:2 * T]).then_inc(s["xnT_out"], 1)
                    act.wait_ge(s["raw_in"], 32 * (i + 1))
                    u = lambda t: t[:, bass.ds(i, 1)].rearrange("k u f -> k (u f)")
                    act.copy(u(w1h), raw_a[:]).then_inc(s["high"], 1)
                    act.copy(w2s[:, bass.ds(i, 1), :, 0:D].rearrange("k u f d -> k (u f) d"), raw_c[:]
                             ).then_inc(s["high"], 1)
                    for j in range(TJ):
                        act.wait_ge(s["shift_done"], TJ * i + j + 1)
                        act.activation(feat[j][:, :, 0:NF], feat[j][:, :, 0:NF], ACT.Exp).then_inc(s["feat_ready"], 1)

                def features_out(j, banks):
                    q_t, k_t = [R[banks[n]][:, 0:NG * P].rearrange("p (g t) -> p g t", g=NG) for n in range(2)]
                    act.wait_ge(s["qT_done"], 4 * i + 2 * j + 1)
                    for r in range(GH):
                        own = slice(32 * r, 32 * r + 32)
                        last = act.activation(qb_t[own, :, j, r], q_t[own], ACT.Identity, bias=eps_col[own, 0:1])
                    if j == 1:
                        last = act.activation(qf_t[:], q_t, ACT.Identity, bias=eps_col[:, 0:1])
                    last.then_inc(s["qT_out"], 1)
                    act.wait_ge(s["qT_done"], 4 * i + 2 * j + 2)
                    act.activation(kf_t[:, :, j * P:(j + 1) * P], k_t, ACT.Identity, bias=eps_col[:, 0:1]
                                   ).then_inc(s["qT_out"], 1)
                if one:
                    if two:
                        act.wait_ge(s["s_done"], 6 * i)
                    features_out(0, (0, 1))
                if tail:
                    act.wait_ge(s["xn2T_done"], i - 1)
                    act.copy(xn2_t[0:KH].rearrange("d c t -> d (c t)"), R[2][0:KH, 0:2 * T]).then_inc(s["xn2T_out"], 1)
                if one:
                    if two:
                        act.wait_ge(s["av_done"], 6 * i)
                    features_out(1, (2, 0))
            sched(act, emit)

        @block.vector
        def _(dve):
            v = nc.vector
            steps = [0]

            def then(ins):
                steps[0] += 1
                ins.then_inc(s["dve_step"], 1)
                dve.wait_ge(s["dve_step"], steps[0])
            dve.wait_ge(s["w_in"], 160)
            then(v.tensor_reduce(top[0:KH, 0:6], omega[:, :, 0:NF], AX, ALU.add))
            then(v.tensor_scalar(omega[:, :, NF], top[0:KH, 0:6], 0.5, None, ALU.mult))
            then(v.memset(count[:], 0.0))
            dve.wait_ge(s["setup"], NSETUP + 4)
            then(v.tensor_reduce(eps_col[:], block_mask[:, :, 0], AX, ALU.add))
            then(v.tensor_scalar(eps_col[:], eps_col[:], EPS_F, None, ALU.mult))

            def norm_stats(src, stats, mv, sem_name, b):
                for j in range(TJ):
                    v.bn_stats(stats[:, j], src[:, j]).then_inc(s[sem_name], 1)
                wait_apart(dve, s[sem_name], 5 * b + 2)
                for j in range(TJ):
                    v.bn_aggr(mv[:, j], stats[:, j]).then_inc(s[sem_name], 1)

            def norm_apply(src, mv, rstd, dst, sem_name, done, rstd_ready, b):
                dve.wait_ge(s[rstd_ready], 2 * (b + 1))
                for j in range(TJ):
                    v.tensor_scalar(dst[:, j], src[:, j], mv[:, j, 0:1], rstd[:, j:j + 1], ALU.subtract, ALU.mult
                                    ).then_inc(s[done if j else sem_name], 1)

            def bc(ap, n):
                return ap.unsqueeze(2).broadcast_to([P, ap.shape[1], n])

            def stats1(b):
                wait_apart(dve, s["h_in"], 16 * (b + 1))
                norm_stats(hb[:, b % 4], stats, mv, "norm_step", b)

            def apply1(b):
                if not (isinstance(b, int) and b == 0):
                    dve.wait_ge(s["xnT_done"], b)
                dve.wait_ge(s["norm_step"], 5 * b + 4)
                norm_apply(hb[:, b % 4], mv, rstd1, xn, "norm_step", "xn_ready", "rstd1_ready", b)

            def feature_scores(i, j):
                sc = R[2 + j][:, 0:2 * H * HW].rearrange("p (h f) -> p h f", f=HW)
                n = 8 * i + 4 * j
                dve.wait_ge(s["qk_done"], TJ * i + j + 1)
                v.tensor_reduce(top[:], sc[:, :, 0:NF], AX, ALU.max).then_inc(s["top_done"], 1)
                dve.wait_ge(s["top_done"], n + 1)
                v.tensor_reduce(top_k[:], top[:, H:], AX, ALU.max).then_inc(s["top_done"], 1)
                v.tensor_tensor(shift[:, 0:H], sc[:, 0:H, NF], top[:, 0:H], ALU.add).then_inc(s["top_done"], 1)
                dve.wait_ge(s["top_done"], n + 3)
                v.tensor_scalar(shift[:, H:], sc[:, H:, NF], top_k[:, 0:1], None, ALU.add).then_inc(s["top_done"], 1)
                dve.wait_ge(s["top_done"], n + 4)
                if not (isinstance(i, int) and i == 0):
                    dve.wait_ge(s["qT_done"], 4 * i - 2 + 2 * j)
                    if j == 0:
                        dve.wait_ge(s["kf_ready"], i)
                v.tensor_tensor(feat[j][:, :, 0:NF], sc[:, :, 0:NF], bc(shift[:], NF), ALU.subtract
                                ).then_inc(s["shift_done"], 1)

            def mask(i, n):
                dve.wait_ge(s["s_done"], 6 * (i - 1) + n + 1)
                if not (isinstance(i, int) and i == 1) or n >= 2:
                    dve.wait_ge(s["av_done"], 6 * (i - 1) + n - 1)
                v.tensor_tensor(masked[n % 2][:], S[n % 2][:], causal[:].unsqueeze(1).broadcast_to([P, GH, P]), ALU.mult
                                ).then_inc(s["s_out"], 1)

            def emit(i, one, two, tail, choice):
                more = one and not (isinstance(i, int) and i == B - 1)
                if two:
                    dve.wait_ge(s["state_done"], i)
                    if not isinstance(i, int) or i >= 2:
                        dve.wait_ge(s["av_done"], 6 * (i - 1))
                    v.tensor_tensor(state[:], M[:, 0:H * VW].rearrange("p (g c) -> p g c", g=NG),
                                    block_mask[:].rearrange("p h v -> p (h v)").unsqueeze(1).broadcast_to([P, NG, GH * VW]),
                                    ALU.mult).then_inc(s["state_out"], 1)
                if more:
                    stats1(i + 1)
                if choice:
                    choose_first(i - 1)
                if two:
                    mask(i, 0)
                    mask(i, 1)
                if one:
                    feature_scores(i, 0)
                if tail:
                    project(i - 1)
                if two:
                    mask(i, 2)
                    mask(i, 3)
                if choice:
                    keep_rows(i - 1)
                if tail:
                    norm2(i - 1)
                if one:
                    dve.wait_ge(s["v_done"], i + 1)
                    if not isinstance(i, int) or i >= 2:
                        dve.wait_ge(s["av_done"], 6 * (i - 1))
                    v.tensor_copy(values[:, i % 2, :, :, 0:DH], R[1][:, 0:TJ * D].rearrange("p (j h d) -> p j h d", j=TJ, h=H)
                                  ).then_inc(s["v_out"], 1)
                    feature_scores(i, 1)
                if two:
                    mask(i, 4)
                    mask(i, 5)
                if more:
                    apply1(i + 1)
                if choice:
                    choose_second(i - 1)
                if two:
                    normalise(i)
                if choice:
                    place(i - 1)
                if tail:
                    gate_logits(i - 1)

            def normalise(i):
                ab = AB[:, 0:TJ * H * VW].rearrange("p (h v) -> p h v", v=VW)
                n = 2 * (i - 1)
                dve.wait_ge(s["av_done"], 6 * i)
                v.tensor_scalar(den[:], ab[:, :, DH], EPS_F * NF, None, ALU.add).then_inc(s["att_step"], 1)
                dve.wait_ge(s["att_step"], n + 1)
                v.reciprocal(den[:], den[:]).then_inc(s["att_step"], 1)
                dve.wait_ge(s["att_step"], n + 2)
                if not isinstance(i, int) or i >= 2:
                    dve.wait_ge(s["attT_done"], i - 1)
                v.tensor_tensor(att[:].rearrange("p j (h d) -> p (j h) d", d=DH), ab[:, :, 0:DH], bc(den[:], DH), ALU.mult
                                ).then_inc(s["att_ready"], 1)

            def project(i):
                par = (i + 1) % 2
                dve.wait_ge(s["proj_done"], i)
                if not isinstance(i, int) or i >= 3:
                    dve.wait_ge(s["h2_stored"], 16 * (i - 2))
                v.tensor_tensor(h2[:, par], hb[:, (i + 3) % 4], R[0][:, 0:TJ * D].rearrange("p (j d) -> p j d", j=TJ), ALU.add
                                ).then_inc(s["h2_ready"], 1)
                wait_apart(dve, s["h2_ready"], i)
                norm_stats(h2[:, par], stats2, mv2, "tail", i - 1)

            def norm2(i):
                if not isinstance(i, int) or i >= 2:
                    dve.wait_ge(s["xn2T_done"], i - 1)
                    dve.wait_ge(s["rows_x"], 4 * (i - 1))
                dve.wait_ge(s["tail"], 5 * (i - 1) + 4)
                norm_apply(h2[:, (i + 1) % 2], mv2, rstd2, xn2, "tail", "xn2_ready", "rstd2_ready", i - 1)

            def gate_logits(i):
                lg = R[3][:, 0:TJ * (NE + 1)].rearrange("p (j e) -> p j e", j=TJ)
                dve.wait_ge(s["logit_done"], i)
                v.tensor_reduce(m[:, 0], lg[:, :, 0:NE], AX, ALU.max).then_inc(s["gate_step"], 1)
                dve.wait_ge(s["gate_step"], 20 * (i - 1) + 1)
                if not isinstance(i, int) or i >= 2:
                    dve.wait_ge(s["prob_ready"], i - 1)
                v.tensor_tensor(logits[:], lg[:, :, 0:NE], bc(m[:, 0], NE), ALU.subtract).then_inc(s["logit_max"], 1)
                v.tensor_scalar(pot[:, bass.ds(i - 1, 1)].rearrange("p b j -> p (b j)"), lg[:, :, NE], -V_MAX, V_MAX, ALU.max, ALU.min).then_inc(s["logit_out"], 1)

            first_w = first[:].unsqueeze(1).broadcast_to([P, TJ, NE])

            def choose_steps(n):
                def step(ins):
                    n[0] += 1
                    ins.then_inc(s["gate_step"], 1)
                    dve.wait_ge(s["gate_step"], n[0])

                def top_of(k):
                    step(v.tensor_reduce(m[:, 2 + k], prob[:], AX, ALU.max))
                    step(v.tensor_tensor(eq[:], prob[:], bc(m[:, 2 + k], NE), ALU.is_equal))
                    step(v.tensor_tensor(w8[:], eq[:], first_w, ALU.mult))
                    step(v.tensor_reduce(m[:, 4], w8[:], AX, ALU.max))
                    step(v.tensor_tensor(pick[k][:], w8[:], bc(m[:, 4], NE), ALU.is_equal))
                return step, top_of

            def choose_first(i):
                step, top_of = choose_steps([20 * (i - 2) + 1])
                dve.wait_ge(s["prob_ready"], i - 1)
                step(v.tensor_reduce(m[:, 1], prob[:], AX, ALU.add))
                step(v.reciprocal(m[:, 1], m[:, 1]))
                step(v.tensor_tensor(prob[:], prob[:], bc(m[:, 1], NE), ALU.mult))
                top_of(0)

            def choose_second(i):
                n = [20 * (i - 2) + 9]
                step, top_of = choose_steps(n)
                step(v.scalar_tensor_tensor(out=prob[:], in0=pick[0][:], scalar=-2.0, in1=prob[:],
                                            op0=ALU.mult, op1=ALU.add))
                top_of(1)
                step(v.tensor_tensor(m[:, 5], m[:, 2], m[:, 3], ALU.add))
                step(v.reciprocal(m[:, 5], m[:, 5]))
                for k in range(2):
                    step(v.tensor_tensor(gate[:, :, k], m[:, 2 + k], m[:, 5], ALU.mult))
                v.tensor_copy(earlier[:, 0], count[:]).then_inc(s["gate_step"], 1)
                step_n = n[0] + 1
                v.tensor_tensor(earlier[:, 1], count[:], pick[0][:, 0], ALU.add).then_inc(s["count_step"], 1)
                v.tensor_tensor(chosen[:], pick[0][:], pick[1][:], ALU.add).then_inc(s["count_step"], 1)
                dve.wait_ge(s["gate_step"], step_n)
                dve.wait_ge(s["count_step"], 3 * (i - 2) + 2)
                v.tensor_tensor(earlier[:, 1], earlier[:, 1], pick[1][:, 0], ALU.add).then_inc(s["count_step"], 1)
                dve.wait_ge(s["count_step"], 3 * (i - 2) + 3)
                v.tensor_tensor(count[:], earlier[:, 1], chosen[:, 1], ALU.add).then_inc(s["chosen_ready"], 1)
                dve.wait_ge(s["chosen_ready"], i - 1)

            def keep_rows(i):
                if not isinstance(i, int) or i >= 3:
                    dve.wait_ge(s["scattered"], 64 * (i - 2))
                for k in range(2):
                    v.tensor_copy(rows[:, :, k, 0:D], xn2[:]).then_inc(s["rows_x"], 1)
                    v.tensor_copy(rows[:, :, k, D:XW], xn2[:, :, P:D]).then_inc(s["rows_x"], 1)

            def place(i):
                n = [6 * (i - 2)]

                def step(ins):
                    n[0] += 1
                    ins.then_inc(s["place_step"], 1)
                    dve.wait_ge(s["place_step"], n[0])
                dve.wait_ge(s["prefix_done"], i - 1)
                v.tensor_tensor(slot_e[:], M[:, 0:TJ * NE].rearrange("p (j e) -> p j e", j=TJ),
                                region[:].unsqueeze(1).broadcast_to([P, TJ, NE]), ALU.add).then_inc(s["slots_ready"], 1)
                dve.wait_ge(s["slots_ready"], i - 1)
                for k in range(2):
                    step(v.tensor_tensor(pick[k][:], pick[k][:], slot_e[:], ALU.mult))
                    step(v.tensor_reduce(slot_f[:, :, k], pick[k][:], AX, ALU.add))
                if not isinstance(i, int) or i >= 3:
                    dve.wait_ge(s["scattered"], 64 * (i - 2))
                v.tensor_copy(slot[:], slot_f[:]).then_inc(s["rows_ready"], 1)
                v.tensor_copy(rows[:, :, :, XW].bitcast(U32), dest[:]).then_inc(s["place_step"], 1)
                n[0] += 1
                v.tensor_copy(rows[:, :, :, XW + 1], gate[:]).then_inc(s["place_step"], 1)
                n[0] += 1
                dve.wait_ge(s["place_step"], n[0])
                v.tensor_scalar(dest[:], dest[:], float(2 * T), None, ALU.add).then_inc(s["rows_ready"], 1)

            stats1(0)
            apply1(0)
            sched(dve, emit)


def experts_block(nc, a, keep, xs_dram, y_dram, v_dram, g_dram):
    ident, count, pot = keep["ident"], keep["count"], keep["pot"]
    FT = FF // P
    HALF = FF // 2
    LANES = 48
    STEPS = 4
    CHAIN_TILES = -(-(T - 1) // STEPS)
    CHAIN_OPS = 3
    with ExitStack() as ctx:
        sb = lambda n, s, d=F32: ctx.enter_context(nc.sbuf_tensor("e_" + n, s, d))
        ps = lambda n, s: ctx.enter_context(nc.psum_tensor("e_" + n, s, F32))
        sem = lambda n: ctx.enter_context(nc.semaphore(n))
        w1h, w1l = (keep[n][:].rearrange("p (e u) f -> p e (u f)", e=NE) for n in ("w1h", "w1l"))
        w1s = sb("w1s", [P, NE, FF], F32R)
        w1x = sb("w1x", [EMB + 2, NE, FF + D], F32R)
        w2s = keep["w2s"][:].rearrange("p (e u) f d -> p e (u f) d", e=NE)
        bias_space = sb("fbias", [P, FF + D])
        bias = bias_space[0:40].bitcast(F32R)
        hid, low = bias_space[:, 0:FF], bias_space[:, FF:]
        raw_w1 = sb("raw_w1", [P, 2, FF])
        free = raw_w1[0:B].rearrange("p e f -> p (e f)")
        z, z2 = (free[:, n * 2 * T:(n + 1) * 2 * T].rearrange("p (c t) -> p c t", c=2) for n in range(2))
        back = free[:, 4 * T:6 * T].rearrange("p (t c) -> p t c", c=2)
        chains = sb("chains", [LANES, 2 * (STEPS * CHAIN_TILES + 1) * 2])
        CL = 2 * (STEPS * CHAIN_TILES + 1)
        chain, chain_a = (chains[:, n * CL:(n + 1) * CL]
                          .rearrange("p (k c) -> p k c", c=2) for n in range(2))
        raw_bias = chains[0:40, 0:FF + D]
        ones = sb("fones", [P, P])
        n_of, n_int = sb("n_of", [P, NE]), sb("n_int", [1, NE], I32)
        tiles_i, tiles_f = sb("tiles_i", [1, NE], I32), sb("tiles_f", [1, NE])
        jump = sb("jump", [1, NE])
        PAD = NE // 2
        sums = [sb(f"sums{n}", [1, PAD + NE]) for n in range(4)]
        zeros = sb("zeros", [P, 1])
        tile_no = sb("tile_no", [1, NTILE + 1])
        ex_f, row_f = sb("ex_f", [1, NTILE + 1]), sb("row_f", [1, NTILE + 1])
        ex_i, row_i = sb("ex_i", [1, NTILE + 1], I32), sb("row_i", [1, NTILE + 1], I32)
        pad_rows, pad_id = sb("pad_rows", [P, ROW]), sb("pad_id", [P, 1], I32)
        x = sb("x", [P, ROW])
        tag = sb("tag", [P, 4, 2])
        gate = sb("slot_gate", [P, 1])
        warm = sb("warm", [1, 1])
        where = sb("where", [P, 1], U32)
        xh, xl = sb("xh", [P, 2, P], F32R), sb("xl", [P, P], F32R)
        bias_rows = sb("bias_rows", [EMB + 2, P], F32R)
        xl1 = sb("xl1", [EMB + 2, P], F32R)
        y = sb("y", [P, D])
        hh, hl = sb("hh", [P, FT, P], F32R), sb("hl", [P, FT, P], F32R)
        pot_t = sb("pot_t", [NT, P])
        v = sb("v", [LANES, T])
        sign = sb("sign", [LANES, T])
        square, size = sb("square", [LANES, 2]), sb("size", [LANES, 1])
        next_a = sb("next_a", [LANES, STEPS, 2])
        state = sb("chain_state", [LANES, STEPS, 2])
        g_out = hid[0:B, 0:2 * T].rearrange("p (c t) -> p c t", c=2)
        XT = ps("xt", [P, 2, P])
        HID = ps("hidden", [P, 2, 512])
        HT = ps("ht", [P, 2, 512])
        Y = ps("yp", [P, 512])
        MISC = ps("fmisc", [P, 512])
        past = HT[0:1].rearrange("p a b -> p (a b)")[:, 0:(NTILE + 1) * NE].rearrange("p (n e) -> p n e", e=NE)

        names = """w_in w_high w_low bias_high consts ones_ready pads_ready bias_moved gelu_loaded rows_set count_done table_ready x_in x_turned x_high x_low
            tagged hid_done hid_ready hidT_done hid_high hid_low y_done low_ready y_ready
            y_out where_ready pads_out pot_done pot_ready v_out step chain_step chain_done g_out pool_step
            bias_in bias_low half_high half_low gate_ready chain_kept chain_set""".split()
        s = {n: sem("f_" + n) for n in names}
        v_in = sem("f_v_in")
        w_in = [sem(f"f_w_in{c}") for c in range(2)]
        block = ctx.enter_context(nc.Block())

        @block.sync
        def _(sp):
            def load_w1(e):
                for r in (0, EMB):
                    sp.dma_start(raw_w1[r:r + EMB, e % 2], a["ew1"][P:D, 2 * e:2 * e + 2].rearrange("k u f -> k (u f)")
                                 ).then_inc(w_in[e % 2], 16)
            load_w1(0)
            load_w1(1)
            sp.wait_ge(s["pads_ready"], 1)
            sp.dma_start(xs_dram[NE * REGION:NSLOT], pad_rows[:]).then_inc(s["pads_out"], 16)
            sp.wait_ge(s["table_ready"], 1)
            for n in range(NE):
                if n >= 2:
                    sp.wait_ge(s["w_low"], n - 1)
                    load_w1(n)
                at = sp.value_load(n_int[0:1, n:n + 1], min_val=0, max_val=B * T)
                sp.dma_start(xs_dram[bass.ds(n * REGION + at, P)], pad_rows[:]).then_inc(s["pads_out"], 16)
            sp.wait_ge(s["table_ready"], 3)
            sp.wait_ge(s["pads_out"], 16 * (NE + 1))

            def load(i):
                at = sp.value_load(row_i[0:1, bass.ds(i, 1)], min_val=0, max_val=NE * REGION)
                sp.dma_start(x[:], xs_dram[bass.ds(at, P)]).then_inc(s["x_in"], 16)
            load(0)
            with sp.Fori(1, NTILE) as i:
                wait_apart(sp, s["x_turned"], i)
                wait_apart(sp, s["tagged"], i)
                load(i)
            sp.wait_ge(s["chain_done"], 1)
            for c in range(2):
                sp.dma_start(g_dram[c], g_out[:, c]).then_inc(s["g_out"], 16)
            sp.wait_ge(s["g_out"], 32)

        @block.gpsimd
        def _(pool):
            g = nc.gpsimd
            g.memset(zeros[:], 0.0).then_inc(s["ones_ready"], 1)
            g.memset(ones[:], 1.0).then_inc(s["ones_ready"], 1)
            g.memset(pad_rows[:], 0.0).then_inc(s["pool_step"], 1)
            g.iota(pad_id[:], [[0, 1]], base=2 * B * T, channel_multiplier=1).then_inc(s["pool_step"], 1)
            for n in range(3):
                g.memset(sums[n][:], 0.0).then_inc(s["consts"], 1)
            g.iota(tile_no[:], [[1, NTILE + 1]], base=0, channel_multiplier=0,
                   allow_small_or_imprecise_dtypes=True).then_inc(s["consts"], 1)
            pool.wait_ge(s["pool_step"], 2)
            g.tensor_copy(pad_rows[:, XW:XW + 1].bitcast(I32), pad_id[:]).then_inc(s["pads_ready"], 1)
            g.memset(v[:], 0.0).then_inc(s["consts"], 1)
            g.memset(raw_bias, 0.0).then_inc(s["consts"], 1)
            pool.wait_ge(s["pot_ready"], 1)
            pool.dma_start(v_dram, pot_t[:]).then_inc(s["v_out"], 16)
            pool.wait_ge(s["v_out"], 16)
            pool.wait_ge(s["consts"], 6)
            for r in (0, 32):
                pool.dma_start(v[r:r + B], v_dram.rearrange("(b j) p -> b (j p)", j=TJ)).then_inc(v_in, 16)
            pool.wait_ge(s["bias_low"], 2)
            for r in range(2):
                pool.dma_start(w1x[EMB + r:EMB + r + 1], bias[32 * r:32 * r + NE]).then_inc(s["bias_moved"], 16)
            pool.wait_ge(s["table_ready"], 3)

            def tag_tile(i):
                wait_apart(pool, s["x_in"], 16 * (i + 1))
                g.tensor_copy(tag[:, i % 4], x[:, XW:]).then_inc(s["tagged"], 1)

            def chain_data(i):
                if not isinstance(i, int) or i >= 2:
                    wait_apart(pool, s["chain_step"], CHAIN_OPS * STEPS * (i - 1))
                    g.tensor_copy(chain[:, bass.ds(STEPS * (i - 2) + 1, STEPS)], state[:]).then_inc(s["chain_kept"], 1)
                g.tensor_copy(next_a[:], chain_a[:, bass.ds(STEPS * (i - 1) + 1, STEPS)]).then_inc(s["chain_kept"], 1)

            def emit(i, front, back_, chained=False):
                if front:
                    tag_tile(i + 1)
                if chained:
                    chain_data(i)
                if back_:
                    if not isinstance(i, int) or i >= 2:
                        wait_apart(pool, s["y_out"], 16 * (i - 1))
                    g.tensor_copy(where[:], tag[:, (i + 3) % 4, 0:1].bitcast(U32)).then_inc(s["where_ready"], 1)
                    pool.wait_ge(s["where_ready"], i)
                    wait_apart(pool, s["y_ready"], i)
                    if not (isinstance(i, int) and i == NTILE):
                        wait_apart(pool, s["tagged"], i + 1)
                        g.tensor_copy(gate[:], tag[:, i % 4, 1:2]).then_inc(s["gate_ready"], 1)
                    pool.indirect_dma_start(out=y_dram, in_=y[:], in_offset=None,
                                            out_offset=bass.IndirectOffsetOnAxis(ap=where[:, 0:1], axis=0)
                                            ).then_inc(s["y_out"], 16)
            tag_tile(0)
            pool.wait_ge(s["tagged"], 1)
            g.tensor_copy(gate[:], tag[:, 0, 1:2]).then_inc(s["gate_ready"], 1)
            emit(0, True, False)
            wait_apart(pool, s["chain_set"], 2)
            emit(1, True, True, True)
            with pool.Fori(2, 1 + CHAIN_TILES) as i:
                emit(i, True, True, True)
            wait_apart(pool, s["chain_step"], CHAIN_OPS * STEPS * CHAIN_TILES)
            g.tensor_copy(chain[:, STEPS * (CHAIN_TILES - 1) + 1:], state[:]).then_inc(s["chain_kept"], 1)
            with pool.Fori(1 + CHAIN_TILES, NTILE - 1) as i:
                emit(i, True, True)
            emit(NTILE - 1, False, True)
            emit(NTILE, False, True)
            pool.wait_ge(s["y_out"], 16 * NTILE)

        @block.tensor
        def _(pe):
            pe.wait_ge(s["ones_ready"], 2)
            pe.matmul(MISC[:, 0:NE], ones[:], count[:], start=True, stop=True).then_inc(s["count_done"], 1)
            pe.transpose(XT[0:NT].rearrange("p a b -> p (a b)")[:, 0:P], pot[:].rearrange("p b j -> p (b j)"), ident[:]
                         ).then_inc(s["pot_done"], 1)
            pe.wait_ge(s["bias_low"], 2)
            pe.wait_ge(s["w_low"], NE)
            pe.wait_ge(s["bias_moved"], 32)
            pe.wait_ge(s["rows_set"], 3)
            pe.wait_ge(s["pot_ready"], 1)

            def turn_x(i):
                pe.wait_ge(s["x_in"], 16 * (i + 1))
                if not (isinstance(i, int) and i == 0):
                    pe.wait_ge(s["x_low"], 2 * i)
                pe.transpose(XT[:, 0], x[:, 0:P], ident[:])
                pe.transpose(XT[:, 1], x[:, P:XW], ident[:]).then_inc(s["x_turned"], 1)
            turn_x(0)

            def emit(i, front, back_, last):
                if front:
                    e = pe.value_load(ex_i[0:1, bass.ds(i, 1)], min_val=0, max_val=NE - 1)
                    pe.wait_ge(s["x_high"], i + 1)
                    pe.wait_ge(s["x_low"], 2 * i + 2)
                    if not (isinstance(i, int) and i == 0):
                        pe.wait_ge(s["hid_ready"], i)
                    for n in range(2):
                        o, c = HID[:, n, 0:HALF], slice(n * HALF, (n + 1) * HALF)
                        w = lambda t, k=P: t[0:k, bass.ds(e, 1), c].rearrange("p e f -> p (e f)")
                        pe.matmul(o, xh[:, 0], w(w1h), start=True, stop=False)
                        pe.matmul(o, xh[:, 0], w(w1l), start=False, stop=False)
                        pe.matmul(o, xl[:], w(w1h), start=False, stop=False)
                        pe.matmul(o, xh[:, 1], w(w1s), start=False, stop=False)
                        mm = pe.matmul(o, xl1[:], w(w1x, EMB + 2), start=False, stop=True)
                    mm.then_inc(s["hid_done"], 1)
                    if not last:
                        turn_x(i + 1)
                if back_:
                    e = pe.value_load(ex_i[0:1, bass.ds(i - 1, 1)], min_val=0, max_val=NE - 1)
                    pe.wait_ge(s["hid_high"], i)
                    pe.wait_ge(s["hid_low"], i)
                    if not isinstance(i, int) or i >= 2:
                        pe.wait_ge(s["y_ready"], i - 1)
                    bias2 = w1x[:, bass.ds(e, 1), FF:].rearrange("p e d -> p (e d)")
                    w = lambda f, n: w2s[:, bass.ds(e, 1), f, 0:n].rearrange("p e d -> p (e d)")
                    for f in range(FT):
                        pe.matmul(Y[:, 0:2 * D], hh[:, f], w(f, 2 * D), start=f == 0, stop=False, skip_group_check=True)
                        pe.matmul(Y[:, 0:D], hl[:, f], w(f, D), start=False, stop=False, skip_group_check=True)
                    pe.matmul(Y[:, 0:D], bias_rows[:], bias2, start=False, stop=True, skip_group_check=True
                              ).then_inc(s["y_done"], 1)
                if front:
                    pe.wait_ge(s["hid_ready"], i + 1)
                    if not (isinstance(i, int) and i == 0):
                        pe.wait_ge(s["hid_low"], i)
                        pe.wait_ge(s["hid_high"], i)
                    for f in range(FT):
                        tr = pe.transpose(HT[:, f // 4, (f % 4) * P:(f % 4 + 1) * P], hid[:, f * P:(f + 1) * P], ident[:])
                    tr.then_inc(s["hidT_done"], 1)
            emit(0, True, False, False)
            emit(1, True, True, False)
            with pe.Fori(2, NTILE - 1) as i:
                emit(i, True, True, False)
            emit(NTILE - 1, True, True, True)
            emit(NTILE, False, True, True)

        @block.scalar
        def _(act):
            act.wait_ge(s["ones_ready"], 2)
            act.activation(warm[:], ones[0:1, 0:1], ACT.Gelu_apprx_tanh).then_inc(s["gelu_loaded"], 1)
            act.wait_ge(s["consts"], 6)
            for r in (0, 32):
                act.dma_start(raw_bias[r:r + NE, 0:FF], a["eb1"]).then_inc(s["bias_in"], 16)
                act.dma_start(raw_bias[r:r + NE, FF:], a["eb2"]).then_inc(s["bias_in"], 16)
            act.wait_ge(s["pot_done"], 1)
            act.copy(pot_t[:], XT[0:NT].rearrange("p a b -> p (a b)")[:, 0:P]).then_inc(s["pot_ready"], 1)
            act.wait_ge(s["gelu_loaded"], 1)
            for e in range(NE):
                act.wait_ge(w_in[e % 2], 32 * (e // 2 + 1))
                act.copy(w1s[:, e], raw_w1[:, e % 2]).then_inc(s["w_high"], 1)
                act.copy(w1x[0:EMB, e, 0:FF], raw_w1[0:EMB, e % 2]).then_inc(s["w_high"], 1)
                if e == 1:
                    act.wait_ge(s["bias_in"], 64)
                    act.copy(bias[:], raw_bias[:]).then_inc(s["bias_high"], 1)
                if e == 3:
                    act.copy(w1x[0:EMB, :, FF:], zeros[0:EMB].unsqueeze(1).broadcast_to([EMB, NE, D])
                             ).then_inc(s["rows_set"], 1)

            def high(i):
                act.wait_ge(s["x_turned"], i + 1)
                if not (isinstance(i, int) and i == 0):
                    act.wait_ge(s["hid_done"], i)
                act.copy(xh[:], XT[:]).then_inc(s["x_high"], 1)
            high(0)

            def emit(i, front, back_, last):
                if front:
                    act.wait_ge(s["hid_done"], i + 1)
                    if not (isinstance(i, int) and i == 0):
                        act.wait_ge(s["hidT_done"], i)
                    act.activation(hid[:].rearrange("p (n f) -> p n f", n=2), HID[:, :, 0:HALF], ACT.Gelu_apprx_tanh
                                   ).then_inc(s["hid_ready"], 1)
                    if not last:
                        high(i + 1)
                if back_:
                    act.wait_ge(s["y_done"], i)
                    act.wait_ge(s["gate_ready"], i)
                    if not isinstance(i, int) or i >= 2:
                        act.wait_ge(s["y_ready"], i - 1)
                    act.activation(low[:], Y[:, D:2 * D], ACT.Copy, scale=gate[:, 0:1]).then_inc(s["low_ready"], 1)
                if front:
                    act.wait_ge(s["hidT_done"], i + 1)
                    if not (isinstance(i, int) and i == 0):
                        act.wait_ge(s["y_done"], i)
                    act.copy(hh[:, 0:4].rearrange("p f t -> p (f t)"), HT[:, 0]).then_inc(s["half_high"], 1)
                    act.copy(hh[:, 4:6].rearrange("p f t -> p (f t)"), HT[:, 1, 0:2 * P]).then_inc(s["hid_high"], 1)
            emit(0, True, False, False)
            emit(1, True, True, False)
            with act.Fori(2, NTILE - 1) as i:
                emit(i, True, True, False)
            emit(NTILE - 1, True, True, True)
            emit(NTILE, False, True, True)

        @block.vector
        def _(dve):
            g = nc.vector
            n_step = [0]

            def then(ins):
                n_step[0] += 1
                ins.then_inc(s["step"], 1)
                dve.wait_ge(s["step"], n_step[0])
            dve.wait_ge(s["count_done"], 1)
            dve.wait_ge(s["consts"], 4)
            then(g.tensor_copy(n_of[:], MISC[:, 0:NE]))
            g.tensor_copy(n_int[:], n_of[0:1]).then_inc(s["table_ready"], 1)
            then(g.tensor_scalar(tiles_f[:], n_of[0:1], float(P - 1), None, ALU.add))
            then(g.tensor_copy(tiles_i[:], tiles_f[:]))
            then(g.tensor_scalar(tiles_i[:], tiles_i[:], 7, None, ALU.logical_shift_right))
            then(g.tensor_copy(sums[0][:, PAD:], tiles_i[:]))
            then(g.tensor_scalar(jump[:], sums[0][:, PAD:], float(-P), float(REGION), ALU.mult, ALU.add))
            for n in range(3):
                then(g.tensor_tensor(sums[n + 1][:, PAD:], sums[n][:, PAD:], sums[n][:, PAD - (1 << n):PAD - (1 << n) + NE],
                                     ALU.add))
            start = sums[3][:, PAD:]
            per_tile = lambda ap: ap.unsqueeze(1).broadcast_to([1, NTILE + 1, NE])
            then(g.tensor_tensor(past[:], tile_no[:].unsqueeze(2).broadcast_to([1, NTILE + 1, NE]), per_tile(start), ALU.is_ge))
            then(g.tensor_reduce(ex_f[:], past[:, :, 0:NE - 1], AX, ALU.add))
            g.tensor_copy(ex_i[:], ex_f[:]).then_inc(s["table_ready"], 1)
            then(g.tensor_tensor(past[:], past[:], per_tile(jump[:]), ALU.mult))
            then(g.tensor_reduce(row_f[:], past[:], AX, ALU.add))
            then(g.scalar_tensor_tensor(out=row_f[:], in0=tile_no[:], scalar=float(P), in1=row_f[:], op0=ALU.mult, op1=ALU.add))
            then(g.tensor_scalar(row_f[:], row_f[:], float(NE * REGION), None, ALU.min))
            g.tensor_copy(row_i[:], row_f[:]).then_inc(s["table_ready"], 1)
            g.tensor_copy(xl1[EMB:], ones[EMB:EMB + 2]).then_inc(s["bias_low"], 1)
            g.tensor_copy(bias_rows[EMB:], ones[EMB:EMB + 2]).then_inc(s["rows_set"], 1)
            g.tensor_copy(bias_rows[0:EMB], zeros[0:EMB].broadcast_to([EMB, P])).then_inc(s["rows_set"], 1)
            for e in range(NE):
                dve.wait_ge(s["w_high"], 2 * e + 2)
                part = w1s[EMB:P, e]
                g.tensor_tensor(part, raw_w1[EMB:P, e % 2], part.bitcast(F32), ALU.subtract).then_inc(s["w_low"], 1)
                if e == 2:
                    dve.wait_ge(s["bias_high"], 1)
                    g.tensor_tensor(bias[32:40], raw_bias[32:40], bias[32:40].bitcast(F32), ALU.subtract
                                    ).then_inc(s["bias_low"], 1)
            dve.wait_ge(s["bias_low"], 2)
            dve.wait_ge(v_in, 32)
            then(g.memset(sign[:], 1.0))
            then(g.memset(sign[:].rearrange("p (k two) -> p k two", two=2)[:, :, 1], -1.0))
            then(g.memset(chain_a[:], -1.0))
            then(g.tensor_scalar(v[:], v[:], -2.0, None, ALU.add))
            then(g.tensor_tensor(chain_a[0:32, 0:T, 0], v[0:32], sign[0:32], ALU.mult))
            then(g.tensor_tensor(chain_a[32:48, 0:T, 0], v[32:48, ::-1], sign[32:48], ALU.mult))
            g.tensor_copy(chain[:, 0], chain_a[:, 0]).then_inc(s["chain_set"], 1)
            g.tensor_copy(state[:, STEPS - 1], chain_a[:, 0]).then_inc(s["chain_set"], 1)
            def low_x(i):
                dve.wait_ge(s["x_high"], i + 1)
                if not (isinstance(i, int) and i == 0):
                    dve.wait_ge(s["hid_done"], i)
                g.tensor_tensor(xl[:], XT[:, 0], xh[:, 0].bitcast(F32), ALU.subtract).then_inc(s["x_low"], 1)
                g.tensor_tensor(xl1[0:EMB], XT[0:EMB, 1], xh[0:EMB, 1].bitcast(F32), ALU.subtract).then_inc(s["x_low"], 1)
            low_x(0)

            def chain_step(i, m):
                n = CHAIN_OPS * (STEPS * (i - 1) + m)
                now, after = state[:, (m - 1) % STEPS], state[:, m]
                if m == 0:
                    dve.wait_ge(s["chain_kept"], 2 * i - 1)
                if m or not isinstance(i, int) or i >= 2:
                    dve.wait_ge(s["chain_step"], n)
                g.tensor_tensor_reduce(out=square[:], in0=now, in1=now, scale=1.0, scalar=0.0,
                                       op0=ALU.mult, op1=ALU.add, accum_out=size[:]).then_inc(s["chain_step"], 1)
                dve.wait_ge(s["chain_step"], n + 1)
                g.reciprocal(size[:], size[:]).then_inc(s["chain_step"], 1)
                dve.wait_ge(s["chain_step"], n + 2)
                g.scalar_tensor_tensor(out=after, in0=now, scalar=size[:, 0:1], in1=next_a[:, m],
                                       op0=ALU.mult, op1=ALU.add).then_inc(s["chain_step"], 1)

            def emit(i, front, back_, last, chained=False):
                if front and not last:
                    low_x(i + 1)
                if chained:
                    chain_step(i, 0)
                    chain_step(i, 1)
                if back_:
                    dve.wait_ge(s["low_ready"], i)
                    if not isinstance(i, int) or i >= 2:
                        dve.wait_ge(s["y_out"], 16 * (i - 1))
                    g.scalar_tensor_tensor(out=y[:], in0=Y[:, 0:D], scalar=gate[:, 0:1], in1=low[:],
                                           op0=ALU.mult, op1=ALU.add).then_inc(s["y_ready"], 1)
                if front:
                    dve.wait_ge(s["half_high"], i + 1)
                    g.tensor_tensor(hl[:, 0:4].rearrange("p f t -> p (f t)"), HT[:, 0],
                                    hh[:, 0:4].rearrange("p f t -> p (f t)").bitcast(F32), ALU.subtract).then_inc(s["half_low"], 1)
                if front:
                    dve.wait_ge(s["hid_high"], i + 1)
                    g.tensor_tensor(hl[:, 4:6].rearrange("p f t -> p (f t)"), HT[:, 1, 0:2 * P],
                                    hh[:, 4:6].rearrange("p f t -> p (f t)").bitcast(F32), ALU.subtract).then_inc(s["hid_low"], 1)
                if chained:
                    chain_step(i, 2)
                    chain_step(i, 3)
            emit(0, True, False, False)
            emit(1, True, True, False, chained=True)
            with dve.Fori(2, 1 + CHAIN_TILES) as i:
                emit(i, True, True, False, chained=True)
            with dve.Fori(1 + CHAIN_TILES, NTILE - 1) as i:
                emit(i, True, True, False)
            emit(NTILE - 1, True, True, True)
            emit(NTILE, False, True, True)
            dve.wait_ge(s["chain_kept"], 2 * CHAIN_TILES)
            then(g.tensor_copy(back, chain[32:48, 0:T][:, ::-1]))
            then(g.tensor_tensor(z[:, 0], chain[0:B, 0:T, 0], back[:, :, 0], ALU.subtract))
            then(g.tensor_tensor(z[:, 0], z[:, 0], sign[0:B], ALU.mult))
            then(g.tensor_tensor(z[:, 0], z[:, 0], v[0:B], ALU.subtract))
            then(g.scalar_tensor_tensor(out=z[:, 1], in0=chain[0:B, 0:T, 1], scalar=1.0, in1=back[:, :, 1],
                                        op0=ALU.add, op1=ALU.add))
            then(g.tensor_tensor(z2, z, z, ALU.mult))
            then(g.tensor_tensor(back[:, :, 0], z2[:, 0], z2[:, 1], ALU.add))
            then(g.reciprocal(back[:, :, 1], back[:, :, 0]))
            then(g.tensor_tensor(g_out[:, 0], z[:, 0], back[:, :, 1], ALU.mult))
            then(g.scalar_tensor_tensor(out=g_out[:, 1], in0=z[:, 1], scalar=-1.0, in1=back[:, :, 1],
                                        op0=ALU.mult, op1=ALU.mult))
            g.tensor_scalar(g_out, g_out, -FEAT_CLAMP, FEAT_CLAMP, ALU.max, ALU.min).then_inc(s["chain_done"], 1)


def output_block(nc, a, h2_dram, y_dram, g_dram, out):
    SLOTS = 4
    GROUPS = B // SLOTS
    with ExitStack() as ctx:
        sb = lambda n, s, d=F32: ctx.enter_context(nc.sbuf_tensor(n, s, d))
        sem = lambda n: ctx.enter_context(nc.semaphore(n))
        w_raw, scale, w = sb("o_w_raw", [3, D]), sb("o_scale", [3, D]), sb("o_w", [3, D])
        gf = [sb(f"o_gf{k}", [3, T]) for k in range(SLOTS)]
        res = [sb(f"o_res{k}", [P, TJ, D]) for k in range(SLOTS)]
        rows = [sb(f"o_rows{k}", [P, TJ, 2, D]) for k in range(SLOTS)]
        spec = [ctx.enter_context(nc.psum_tensor(f"o_spec{k}", [P, TJ, D + EMB], F32)) for k in range(SLOTS)]
        w_in, ones_ready, w_ready = sem("o_w_in"), sem("o_ones_ready"), sem("o_w_ready")
        loaded = [sem(f"o_loaded{k}") for k in range(SLOTS)]
        spec_done, half_done, sum_done = sem("o_spec_done"), sem("o_half_done"), sem("o_sum_done")
        out_done = [sem(f"o_out_done{k}") for k in range(SLOTS)]
        other_done = sem("o_other_done")
        block = ctx.enter_context(nc.Block())
        y_view = y_dram[0:2 * B * T].rearrange("(b j p k) d -> b p j (k d)", j=TJ, p=P, k=2)
        out_view = out.rearrange("b (j p) d -> b p j d", j=TJ)

        @block.sync
        def _(sp):
            sp.dma_start(w_raw[:], a["out_wb"]).then_inc(w_in, 16)
            sp.dma_start(scale[:], a["bk_scale"].broadcast_to([3, D])).then_inc(w_in, 16)
            sp.wait_ge(ones_ready, SLOTS)

            def group(n, later):
                for k in range(SLOTS):
                    b = n * SLOTS + k
                    one = lambda t: t[bass.ds(b, 1)]
                    if later:
                        sp.wait_ge(out_done[k], 16 * n)
                    sp.dma_start(res[k][:], h2_dram[:, bass.ds(b, 1)].rearrange("p b (j d) -> p (b j) d", j=TJ)
                                 ).then_inc(loaded[k], 16)
                    sp.dma_start(rows[k][:].rearrange("p j k d -> p j (k d)"),
                                 one(y_view).rearrange("b p j d -> (b p) j d")).then_inc(loaded[k], 16)
                    sp.dma_start(gf[k][0:2], g_dram[:, bass.ds(b, 1)].rearrange("c b t -> (c b) t")
                                 ).then_inc(loaded[k], 16)
            group(0, False)
            with sp.Fori(1, GROUPS) as n:
                group(n, True)

        @block.gpsimd
        def _(pool):
            for k in range(SLOTS):
                nc.gpsimd.memset(gf[k][:], 1.0).then_inc(ones_ready, 1)
            with pool.Fori(0, GROUPS) as n:
                for k in range(SLOTS):
                    pool.wait_ge(loaded[k], 48 * (n + 1))
                    nc.gpsimd.tensor_tensor(res[k][:], res[k][:], rows[k][:, :, 0], ALU.add).then_inc(half_done, 1)

        @block.tensor
        def _(pe):
            pe.wait_ge(w_ready, 1)

            def group(n, later):
                for k in range(SLOTS):
                    pe.wait_ge(loaded[k], 48 * (n + 1))
                    if later:
                        pe.wait_ge(out_done[k], 16 * n)
                    for j in range(TJ):
                        mm = pe.matmul(spec[k][:, j, 0:D], gf[k][:, j * P:(j + 1) * P], w[:], start=True, stop=True)
                    mm.then_inc(spec_done, 1)
            group(0, False)
            with pe.Fori(1, GROUPS) as n:
                group(n, True)

        @block.vector
        def _(dve):
            dve.wait_ge(w_in, 32)
            nc.vector.tensor_tensor(w[:], w_raw[:], scale[:], ALU.mult).then_inc(w_ready, 1)
            with dve.Fori(0, GROUPS) as n:
                for k in range(SLOTS):
                    c = n * SLOTS + k + 1
                    dve.wait_ge(spec_done, c)
                    nc.vector.tensor_tensor(rows[k][:, :, 1], rows[k][:, :, 1], spec[k][:, :, 0:D], ALU.add
                                            ).then_inc(other_done, 1)
                    dve.wait_ge(half_done, c)
                    dve.wait_ge(other_done, c)
                    nc.vector.tensor_tensor(res[k][:], res[k][:], rows[k][:, :, 1], ALU.add).then_inc(sum_done, 1)

        @block.scalar
        def _(act):
            with act.Fori(0, GROUPS) as n:
                for k in range(SLOTS):
                    act.wait_ge(sum_done, n * SLOTS + k + 1)
                    act.dma_start(out_view[bass.ds(n * SLOTS + k, 1)].rearrange("b p j d -> (b p) j d"), res[k][:]
                                  ).then_inc(out_done[k], 16)
            for k in range(SLOTS):
                act.wait_ge(out_done[k], 16 * GROUPS)


def vit_layer(nc, a, out):
    scratch = lambda n, shape: nc.dram_tensor(n, shape, F32).ap()
    h_dram, h2_dram = scratch("h_dram", (P, B, TJ * D)), scratch("h2_dram", (P, B, TJ * D))
    xs_dram = scratch("xs_dram", (NSLOT, ROW))
    y_dram = scratch("y_dram", (2 * B * T + P, D))
    v_dram, g_dram = scratch("v_dram", (NT, P)), scratch("g_dram", (2, B, T))
    with ExitStack() as ctx:
        sb = lambda n, s: ctx.enter_context(nc.sbuf_tensor(n, s, F32))
        ident = sb("ident", [P, P])
        count = sb("count", [P, NE])
        pot = sb("pot", [P, B, TJ])
        tokens_block(nc, a, ident, h_dram)
        keep = dict(ident=ident, count=count, pot=pot, **expert_weights(nc, ctx))
        attention_block(nc, a, keep, h_dram, h2_dram, xs_dram)
        experts_block(nc, a, keep, xs_dram, y_dram, v_dram, g_dram)
        output_block(nc, a, h2_dram, y_dram, g_dram, out)


def layouts(i):
    c = np.ascontiguousarray
    x = i["x"]
    o = {}
    for n, p in enumerate((1, 2, 4)):
        g = 64 // p
        o[f"x{n}"] = c(x.reshape(B, 3, g, p, g, p).transpose(2, 4, 0, 3, 5, 1).reshape(g * g, B * p * p * 3))
    o["idx"] = c(np.concatenate([i["L0_tok_idx0"].reshape(2, P, 16).transpose(1, 0, 2).reshape(P, 32),
                                 i["L0_tok_idx1"].reshape(64, 2, 8).transpose(1, 0, 2).reshape(P, 8),
                                 i["L0_tok_idx2"].reshape(16, 8, 2).transpose(1, 0, 2).reshape(P, 2)], 1))
    o["w0"] = c(i["L0_tok_W0"].T)
    o["w1"] = c(i["L0_tok_W1"].T.reshape(2, KH, EMB).transpose(1, 0, 2))
    o["w2"] = c(i["L0_tok_W2"].T.reshape(16, 48, EMB).transpose(1, 0, 2))
    o["tok_b"] = c(np.stack([i[f"L0_tok_b{n}"] for n in range(3)], 1))
    o["wf"] = c(i["L0_tok_Wf"].T)
    o["bf"] = i["L0_tok_bf"].reshape(1, D)
    o["up1"] = upsampling(64)
    o["up2"] = np.concatenate([upsampling(16), np.ones((1, T), np.float32)])
    w, b = i["L0_attn_w_inp"][0], i["L0_attn_b_inp"]
    o["wqk_t"] = c(np.concatenate([w.T, b[:, None]], 1)[:2 * D].reshape(4, KH, D + 1).transpose(1, 0, 2))

    def halves(w, b):
        n = w.shape[1]
        return np.concatenate([w.reshape(2, KH, n).transpose(1, 0, 2), np.broadcast_to(b, (1, 2, n))], 0)
    o["wv"] = halves(w[:, 2 * D:], b[2 * D:])
    o["w_out"] = halves(i["L0_attn_w_out"][0], i["L0_attn_b_out"])
    o["w_gate"] = halves(np.concatenate([i["L0_ffn_gate_w"], i["L0_ffn_v_w"][:, None]], 1),
                         np.append(i["L0_ffn_gate_b"], i["L0_ffn_v_b"]))
    o["omega_t"] = c(i["L0_attn_omega"].T)
    o["ew1"] = i["L0_ffn_w1"].transpose(1, 0, 2).reshape(D, UNITS, UF)
    o["ew2"] = i["L0_ffn_w2"].reshape(NE, FF // P, P, D).transpose(2, 0, 1, 3).reshape(P, UNITS, UT, D)
    o["eb1"], o["eb2"] = i["L0_ffn_b1"], i["L0_ffn_b2"]
    o["out_wb"] = np.concatenate([i["L0_ffn_out_w"], i["L0_ffn_out_b"][None]])
    o["bk_scale"] = i["L0_ffn_bk_scale"].reshape(1, D)
    return {n: c(v) for n, v in o.items()}


def kernel(**inputs):
    import concourse.bacc as bacc
    from concourse.bass_utils import run_bass_kernel_spmd

    nc = bacc.Bacc("TRN2", target_bir_lowering=False, num_devices=1)
    arrays = layouts({n: np.asarray(v) for n, v in inputs.items()})
    a = {n: nc.dram_tensor("in_" + n, v.shape, mybir.dt.from_np(v.dtype), kind="ExternalInput").ap()
         for n, v in arrays.items()}
    out = nc.dram_tensor("result", (B, T, D), F32, kind="ExternalOutput").ap()
    vit_layer(nc, a, out)
    r = run_bass_kernel_spmd(nc, [{"in_" + n: v for n, v in arrays.items()}], core_ids=[0])
    return r.results[0]["result"]
```
